# Optimizing a Trainium2 kernel written in Bass

```python
import numpy as np
import jax
import jax.numpy as jnp

def _softmax(x, axis=-1):
    return jax.nn.softmax(x, axis=axis)

def _gelu(x):
    return jax.nn.gelu(x, approximate=True)

def _silu(x):
    return jax.nn.silu(x)

def _sigmoid(x):
    return jax.nn.sigmoid(x)

def _layernorm(x, axis=-1, eps=1e-05):
    m = jnp.mean(x, axis=axis, keepdims=True)
    v = jnp.var(x, axis=axis, keepdims=True)
    return (x - m) / jnp.sqrt(v + eps)

def _scatter_add(tgt, idx, src, axis=0):
    return tgt.at[idx].add(src)

def _segment_sum(src, seg, n):
    return jax.ops.segment_sum(src, seg, n)
kernel_name = 'mk_xattn_ffn_d1_seqx_r8_70d7e3'

def setup_inputs(seed: int=0):
    np.random.seed(seed)
    _w = jnp.asarray

    def _rec_inputs():
        import jax
        import jax.numpy as jnp
        _rk = jax.random.key(seed)
        x = -0.0003929 + 0.9999 * jax.random.normal(jax.random.fold_in(_rk, 1), (128, 64, 128), jnp.float32)
        _lenS = 64 - jax.random.randint(jax.random.fold_in(_rk, 7), (128,), 0, max(1, 64 // 4) + 1, jnp.int32)
        _lenS2 = 64 - jax.random.randint(jax.random.fold_in(_rk, 8), (128,), 0, max(1, 64 // 4) + 1, jnp.int32)
        _ctx_1024P = jax.random.normal(jax.random.fold_in(_rk, 11), (128, 16, 128), jnp.float32)
        _ctx_1024c = jax.random.dirichlet(jax.random.fold_in(_rk, 511), 0.3 * jnp.ones((16,), jnp.float32), (128, 64))
        _ctx_1024t = jnp.einsum('bsk,bkd->bsd', _ctx_1024c, _ctx_1024P)
        _ctx_1024t = _ctx_1024t * jax.lax.rsqrt(jnp.mean(jnp.square(_ctx_1024t)) + 1e-12) * 0.953939
        ctx_1024 = 2.81802e-05 + 1.00001 * (_ctx_1024t + 0.3 * jax.random.normal(jax.random.fold_in(_rk, 611), (128, 64, 128), jnp.float32))
        return (x, ctx_1024)
    x, ctx_1024 = _rec_inputs()

    def _L0_xattn_setup():
        import jax, jax.numpy as jnp
        import numpy as np
        EPS = 1e-08
        LN_EPS = 1e-05

        def _layernorm(x, g, b):
            mu = jnp.mean(x, axis=-1, keepdims=True)
            var = jnp.var(x, axis=-1, keepdims=True)
            return (x - mu) * jax.lax.rsqrt(var + LN_EPS) * g + b

        def _prob(x):
            x = jnp.tanh(x) * 0.499 + 0.5
            return jnp.clip(x / (jnp.sum(x, axis=-1, keepdims=True) + EPS), EPS)
        key = jax.random.key(seed)
        ks = jax.random.split(key, 8)
        B, N, D = (8, 256, 128)
        H = 4 * D
        s = 0.02
        return {'q': jax.random.normal(ks[0], (B, N, D), jnp.float32), 'k': jax.random.normal(ks[1], (B, N, D), jnp.float32), 'v': jax.random.normal(ks[2], (B, N, D), jnp.float32), 'W_diff': jax.random.normal(ks[3], (D, D), jnp.float32) * s, 'b_diff': jnp.zeros((D,), jnp.float32), 'ln_g': jnp.ones((D,), jnp.float32), 'ln_b': jnp.zeros((D,), jnp.float32), 'W1': jax.random.normal(ks[4], (H, D), jnp.float32) * s, 'b1': jnp.zeros((H,), jnp.float32), 'W2': jax.random.normal(ks[5], (D, H), jnp.float32) * s, 'b2': jnp.zeros((D,), jnp.float32)}
    _L0_xattn_all = _L0_xattn_setup()
    _L0_xattn_in = {k: v for k, v in _L0_xattn_all.items() if k in ('W_diff', 'b_diff', 'ln_g', 'ln_b', 'W1', 'b1', 'W2', 'b2')}
    del _L0_xattn_all

    def _L0_ffn_setup():
        import jax, jax.numpy as jnp
        import numpy as np
        FP8_MAX = 448.0
        SCALE = 1.0
        _FP8_DTYPE = getattr(jnp, 'float8_e4m3fn', jnp.float16)

        def quantize_e4m3(t, scale):
            return jnp.clip(t / scale, -FP8_MAX, FP8_MAX).astype(_FP8_DTYPE)
        key = jax.random.key(seed)
        kx, kw = jax.random.split(key)
        B, N, C, F = (8, 512, 128, 128)
        x = jax.random.normal(kx, (B, N, C), dtype=jnp.float32)
        weight = jax.random.normal(kw, (F, C), dtype=jnp.float32) * 0.02
        bias = jnp.zeros((F,), dtype=jnp.float32)
        return {'x': x, 'weight': weight, 'bias': bias}
    _L0_ffn_all = _L0_ffn_setup()
    _L0_ffn_in = {k: v for k, v in _L0_ffn_all.items() if k in ('weight', 'bias')}
    del _L0_ffn_all
    return {'x': x, 'ctx_1024': ctx_1024, 'L0_xattn_W_diff': _L0_xattn_in['W_diff'], 'L0_xattn_b_diff': _L0_xattn_in['b_diff'], 'L0_xattn_ln_g': _L0_xattn_in['ln_g'], 'L0_xattn_ln_b': _L0_xattn_in['ln_b'], 'L0_xattn_W1': _L0_xattn_in['W1'], 'L0_xattn_b1': _L0_xattn_in['b1'], 'L0_xattn_W2': _L0_xattn_in['W2'], 'L0_xattn_b2': _L0_xattn_in['b2'], 'L0_ffn_weight': _L0_ffn_in['weight'], 'L0_ffn_bias': _L0_ffn_in['bias']}

def reference(x, ctx_1024, L0_xattn_W_diff, L0_xattn_b_diff, L0_xattn_ln_g, L0_xattn_ln_b, L0_xattn_W1, L0_xattn_b1, L0_xattn_W2, L0_xattn_b2, L0_ffn_weight, L0_ffn_bias):
    import jax
    import jax.numpy as jnp

    def _L0_xattn_ref(q, k, v, W_diff, b_diff, ln_g, ln_b, W1, b1, W2, b2):
        import jax, jax.numpy as jnp
        import numpy as np
        EPS = 1e-08
        LN_EPS = 1e-05

        def _layernorm(x, g, b):
            mu = jnp.mean(x, axis=-1, keepdims=True)
            var = jnp.var(x, axis=-1, keepdims=True)
            return (x - mu) * jax.lax.rsqrt(var + LN_EPS) * g + b

        def _prob(x):
            x = jnp.tanh(x) * 0.499 + 0.5
            return jnp.clip(x / (jnp.sum(x, axis=-1, keepdims=True) + EPS), EPS)
        D = q.shape[-1]
        q_prob = _prob(q)
        k_prob = _prob(k)
        log_ratio = jnp.log(q_prob) - jnp.log(k_prob)
        sid = jnp.einsum('bnd,bmd->bnm', q_prob - k_prob, log_ratio)
        sid_sim = -sid
        attn = jax.nn.softmax(sid_sim / D ** 0.5, axis=-1)
        attn_feat = jnp.einsum('bnm,bmd->bnd', attn, v)
        f_diff = (v - attn_feat) @ W_diff.T + b_diff + q
        h = _layernorm(f_diff, ln_g, ln_b)
        mlp = jax.nn.gelu(h @ W1.T + b1, approximate=False) @ W2.T + b2
        out = mlp + f_diff
        return _layernorm(out, ln_g, ln_b)

    def _L0_ffn_ref(x, weight, bias):
        import jax, jax.numpy as jnp
        import numpy as np
        FP8_MAX = 448.0
        SCALE = 1.0
        _FP8_DTYPE = getattr(jnp, 'float8_e4m3fn', jnp.float16)

        def quantize_e4m3(t, scale):
            return jnp.clip(t / scale, -FP8_MAX, FP8_MAX).astype(_FP8_DTYPE)
        B, N, C = x.shape
        x2d = x.reshape(B * N, C)
        x_mat = quantize_e4m3(x2d, SCALE).astype(jnp.float16)
        w_mat = quantize_e4m3(weight, SCALE).astype(jnp.float16)
        out2d = (x_mat @ w_mat.T).astype(jnp.float32) * (SCALE * SCALE)
        out2d = out2d + bias
        return out2d.reshape(B, N, -1)
    x = x + _L0_xattn_ref(_layernorm(x, axis=-1), ctx_1024, ctx_1024, L0_xattn_W_diff, L0_xattn_b_diff, L0_xattn_ln_g, L0_xattn_ln_b, L0_xattn_W1, L0_xattn_b1, L0_xattn_W2, L0_xattn_b2)
    x = x + _L0_ffn_ref(_layernorm(x, axis=-1), L0_ffn_weight, L0_ffn_bias)
    return x

_drawn_inputs = setup_inputs


def setup_inputs(seed=0):
    import zlib

    import numpy as np

    out = dict(_drawn_inputs(seed))
    spreads = {'L0_xattn_b_diff': (0.0, 0.1),
     'L0_xattn_ln_g': (1.0, 0.2),
     'L0_xattn_ln_b': (0.0, 0.1),
     'L0_xattn_b1': (0.0, 0.735),
     'L0_xattn_b2': (0.0, 0.1),
     'L0_ffn_bias': (0.0, 0.1)}
    factors = {}
    for name, (base, spread) in spreads.items():
        noise = np.random.default_rng([zlib.crc32(name.encode()), seed]).standard_normal(out[name].shape)
        drawn = base * np.exp(spread * noise) if base else spread * noise
        out[name] = jnp.asarray(drawn.astype(out[name].dtype))
    for name, factor in factors.items():
        out[name] = (out[name] * factor).astype(out[name].dtype)
    return out
```

```python
from contextlib import ExitStack

import concourse.bass as bass
from concourse import mybir

F32 = mybir.dt.float32
F32R = mybir.dt.float32r
BF16 = mybir.dt.bfloat16
F16 = mybir.dt.float16
F8 = mybir.dt.float8e4
ALU = mybir.AluOpType
ACT = mybir.ActivationFunctionType
AX = mybir.AxisListType

P = 128
LN_EPS = 1e-5
PROB_EPS = 1e-8
TANH_GAIN, TANH_SHIFT = 0.499, 0.5
E4M3FN_MAX = 448.0
E4M3_SAFE = 128.0


class Chunk:

    def __init__(self, half, odd, lag, chunks):
        self.n = 2 * half + (odd - lag)
        self.pair = half + (odd - lag) // 2
        self.buf = (odd - lag) % 2
        self.live = not isinstance(half, int) or 0 <= self.n < chunks


def wait(eng, sem, count):
    if isinstance(count, int) and count <= 0:
        return
    eng.wait_ge(sem, count)


def run_steps(eng, chunks, last_lag, step):
    first = (last_lag + 2) // 2
    for n in range(2 * first):
        step(lambda lag, n=n: Chunk(n // 2, n % 2, lag, chunks))
    with eng.Fori(first, chunks // 2) as half:
        for odd in range(2):
            step(lambda lag, odd=odd: Chunk(half, odd, lag, chunks))
    for n in range(chunks, chunks + last_lag):
        step(lambda lag, n=n: Chunk(n // 2, n % 2, lag, chunks))


def xattn_ffn_kernel(nc, x, ctx_in, W_diff, b_diff, ln_g, ln_b, W1, b1, W2, b2, Wf, bf, out):
    B, S, D = x.shape
    HID = W1.shape[0]
    HB = HID // P
    assert D == P and 2 * S == P
    T = B * S // P
    G = 4
    C = G * D
    NC = T // G
    EPW = 256

    x_d = x.rearrange("b s d -> (b s) d").rearrange("(c t p) d -> c p t d", t=G, p=P)
    ctx_d = ctx_in.rearrange("b s d -> (b s) d").rearrange("(c t p) d -> c p t d", t=G, p=P)
    out_d = out.rearrange("b s d -> (b s) d").rearrange("(c t p) d -> c p t d", t=G, p=P)

    with ExitStack() as ctx:
        def sb(name, shape, dt=F32):
            return ctx.enter_context(nc.sbuf_tensor(name, shape, dt))

        def sem(name):
            return ctx.enter_context(nc.semaphore(name))

        bank = [ctx.enter_context(nc.psum_tensor(f"bank{i}", [P, 512], F32)) for i in range(8)]

        X = sb("X", [P, T * D])
        TQ = sb("TQ", [P, T * D])
        TK = sb("TK", [P, T * D])
        F = sb("F", [P, T * D])
        PV = sb("PV", [P, T * (D + 1)])
        SUM = sb("SUM", [P, 2 * T])
        SUMQ, SUMK = SUM[:, 0:T], SUM[:, T:2 * T]
        NORM = sb("NORM", [P, 2 * T])
        RNORM = sb("RNORM", [P, 2 * T])
        GAINS = sb("GAINS", [P, 2 * T])
        SHIFT = sb("SHIFT", [P, T])
        NRATIO = sb("NRATIO", [P, T])
        LRATIO = sb("LRATIO", [P, T])
        SSF = sb("SSF", [P, T])
        RSTDF = sb("RSTDF", [P, T])

        ident = sb("ident", [P, P])
        ident8 = sb("ident8", [P, P], F8)
        half_c = sb("half_c", [P, 1])
        pow_c = sb("pow_c", [P, G])
        WdT = sb("WdT", [P, D])
        W1h = sb("W1h", [P, HID], F32R)
        W1l = sb("W1l", [P, HID], F32R)
        b1c = sb("b1c", [P, HB])
        W2T = sb("W2T", [P, HB * D])
        WfT = sb("WfT", [P, D], BF16)
        rows = sb("rows", [P, 5 * D])
        bd_r, g_r, b_r, b2_r, bf_r = (rows[:, i * D:(i + 1) * D] for i in range(5))
        g_col = sb("g_col", [P, 1])
        b_col = sb("b_col", [P, 1])

        ctx_c = sb("ctx_c", [P, 2 * C])
        q_c = sb("q_c", [P, 2 * C])
        vT_c = sb("vT_c", [P, 2 * C])
        lnq_c, diff_c, dT_c = ctx_c, q_c, vT_c
        lr_c = sb("lr_c", [P, 2 * C])
        lT_c = sb("lT_c", [P, 2 * C])
        E_c = sb("E_c", [P, 2 * C])
        junk = sb("junk", [P, C], BF16)
        hTh = sb("hTh", [P, 2 * C], F32R)
        hTl = sb("hTl", [P, 2 * C], F32R)
        xstat = sb("xstat", [P, 2 * G * 6])
        xmv = sb("xmv", [P, 2 * G * 2])
        xgap = sb("xgap", [P, 2 * G])
        xvar = sb("xvar", [P, 2 * G])
        xrstd = sb("xrstd", [P, 2 * G])
        fvar = sb("fvar", [P, 2 * G])
        nrden = sb("nrden", [P, 2 * G])
        sso = sb("sso", [P, 2 * G])
        ovar = sb("ovar", [P, 2 * G])
        orstd = sb("orstd", [P, 2 * G])

        hid_c = TQ[:, 0:2 * HB * C]
        x1_c = TQ[:, 8 * C:10 * C]
        y_c = TQ[:, 10 * C:12 * C]
        h_c, o_c, xb_c, f2_c = (TK[:, 2 * i * C:2 * (i + 1) * C] for i in range(4))
        xq_c = PV[:, 0:C // 2].bitcast(F8)
        xqT_c = PV[:, C:2 * C].bitcast(BF16)
        r16_c = PV[:, 2 * C:3 * C].bitcast(F16)
        FREE_AT = 12

        Wd_raw = E_c[:, 0:D]
        W1_raw = lr_c[:, 0:HB * D]
        W2_raw = lT_c[:, 0:HID]
        Wf_raw = E_c[:, D:2 * D]
        wq = [E_c[:, (2 + i) * D:(3 + i) * D] for i in range(5)]
        Wcol = lT_c[:, C:C + HB + 1]
        W1g = lr_c[:, C:C + HID]
        raw8 = junk[:, 0:D].bitcast(F8)

        def chunk(t, k, width=C):
            return t[:, bass.ds(k.n * width, width)] if not isinstance(k.n, int) else t[:, k.n * width:(k.n + 1) * width]

        def buf(t, k, width=C):
            return t[:, k.buf * width:(k.buf + 1) * width]

        def tile(t, k, i):
            return t[:, k.buf * C + i * D:k.buf * C + (i + 1) * D]

        def tiles(ap):
            return ap.rearrange("p (t d) -> p t d", d=D)

        def per_tile(t, k, i=0, n=G):
            at = k.n * G + i
            return t[:, bass.ds(at, n)] if not isinstance(at, int) else t[:, at:at + n]

        def all_tile(t, k, i, width=D, stride=D):
            at = (k.n * G + i) * stride
            return t[:, bass.ds(at, width)] if not isinstance(at, int) else t[:, at:at + width]

        def over_tiles(row):
            return row.unsqueeze(1).broadcast_to([P, G, D])

        def over_features(col):
            return col.unsqueeze(2).broadcast_to([P, G, D])

        def pv_chunk(k):
            w = D + 1
            at = k.n * G * w
            ap = PV[:, bass.ds(at, G * w)] if not isinstance(at, int) else PV[:, at:at + G * w]
            return ap.rearrange("p (t w) -> p t w", w=w)[:, :, 0:D]

        w_in, consts, w_tp, w_sb, w_done = sem("w_in"), sem("consts"), sem("w_tp"), sem("w_sb"), sem("w_done")
        wv, wfq, b1_ps, b1_sb, w1_sb = sem("wv"), sem("wfq"), sem("b1_ps"), sem("b1_sb"), sem("w1_sb")
        x_in = [sem(f"x_in{i}") for i in range(2)]
        ctx_sem = [sem(f"ctx_in{i}") for i in range(2)]
        x_bn, x_halves, x_terms = sem("x_bn"), sem("x_halves"), sem("x_terms")
        x_var, x_rstd = sem("x_var"), sem("x_rstd")
        q_ready, qb_ready, pq_ready = sem("q_ready"), sem("qb_ready"), sem("pq_ready")
        tanh_k, tanh_q, ksum = sem("tanh_k"), sem("tanh_q"), sem("ksum")
        vT_ps, vT_sb, P_ps, P_sb = sem("vT_ps"), sem("vT_sb"), sem("P_ps"), sem("P_sb")
        norms, lratio = sem("norms"), sem("lratio")
        kscaled = sem("kscaled")
        kpart, ln_ready, diff_ready, lr_ready = sem("kpart"), sem("ln_ready"), sem("diff_ready"), sem("lr_ready")
        dT_ps, dT_sb, lT_ps, lT_sb = sem("dT_ps"), sem("dT_sb"), sem("lT_ps"), sem("lT_sb")
        s_ps, e_ready, ep_ps, rden, f_ready = sem("s_ps"), sem("e_ready"), sem("ep_ps"), sem("rden"), sem("f_ready")
        ssf_ready, fvar_ready, frstd = sem("ssf_ready"), sem("fvar_ready"), sem("frstd")
        h_ready, hT_ps, hi_ready, lo_ready = sem("h_ready"), sem("hT_ps"), sem("hi_ready"), sem("lo_ready")
        m1_ps, gelu_ready, m2_ps, o_ready = sem("m1_ps"), sem("gelu_ready"), sem("m2_ps"), sem("o_ready")
        f2_ready, xb_ready, sso_ready, ovar_ready, orstd_ready = (
            sem("f2_ready"), sem("xb_ready"), sem("sso_ready"), sem("ovar_ready"), sem("orstd_ready"))
        xn_ready, x1_ready, x1_bn, x1_halves, x1_terms, x1_var, x1_rstd = (
            sem("xn_ready"), sem("x1_ready"), sem("x1_bn"), sem("x1_halves"), sem("x1_terms"), sem("x1_var"),
            sem("x1_rstd"))
        x1b_ready, xq_ready, xqT_ps, xqT_sb, ff_ps, r16_ready, y_ready = (
            sem("x1b_ready"), sem("xq_ready"), sem("xqT_ps"), sem("xqT_sb"), sem("ff_ps"), sem("r16_ready"),
            sem("y_ready"))
        stored = [sem(f"stored{i}") for i in range(2)]

        WEIGHT_LOADS = 12
        NORM_STEPS = 7
        block = ctx.enter_context(nc.Block())

        @block.sync
        def _(sp):
            def load(k):
                wait(sp, x_var, k.n - 1)
                sp.dma_start(tiles(chunk(X, k)), x_d[k.n]).then_inc(x_in[k.buf], 16)
                wait(sp, tanh_k, k.n - 1)
                wait(sp, vT_ps, k.n - 1)
                sp.dma_start(tiles(buf(ctx_c, k)), ctx_d[k.n]).then_inc(ctx_sem[k.buf], 16)

            for n in range(2):
                load(Chunk(0, n, 0, NC))
            sp.dma_start(Wd_raw, W_diff).then_inc(w_in, 16)
            sp.dma_start(W1_raw.rearrange("p (j d) -> p j d", d=D),
                         W1.rearrange("(j p) d -> p j d", p=P)).then_inc(w_in, 16)
            sp.dma_start(W2_raw, W2).then_inc(w_in, 16)
            sp.dma_start(Wf_raw, Wf).then_inc(w_in, 16)
            for row, vec in ((bd_r, b_diff), (g_r, ln_g), (b_r, ln_b), (b2_r, b2), (bf_r, bf)):
                sp.dma_start(row, vec.unsqueeze(0).broadcast_to([P, D])).then_inc(w_in, 16)
            sp.dma_start(g_col[:, :], ln_g.unsqueeze(1), allow_slow_non_contiguous=True).then_inc(w_in, 16)
            sp.dma_start(b_col[:, :], ln_b.unsqueeze(1), allow_slow_non_contiguous=True).then_inc(w_in, 16)
            sp.dma_start(Wcol[:, 0:HB], b1.rearrange("(j p) -> p j", p=P),
                         allow_slow_non_contiguous=True).then_inc(w_in, 16)
            with sp.Fori(1, NC // 2) as half:
                for odd in range(2):
                    load(Chunk(half, odd, 0, NC))

            def store(k):
                wait(sp, y_ready, k.n + 1)
                sp.dma_start(out_d[k.n], tiles(buf(y_c, k))).then_inc(stored[k.buf], 16)

            with sp.Fori(0, NC // 2) as half:
                for odd in range(2):
                    store(Chunk(half, odd, 0, NC))
            for s in stored:
                sp.wait_ge(s, 16 * (NC // 2))

        @block.gpsimd
        def _(pool):
            pool.memset(ident[:, :], 0.0).then_inc(consts, 1)
            pool.memset(pow_c[:, :], -0.5).then_inc(consts, 1)
            pool.wait_ge(consts, 2)
            pool.affine_select(out=ident[:, :], in_=ident[:, :], compare_op=ALU.not_equal, fill=1.0,
                               base=0, pattern=[[-1, P]], channel_multiplier=1).then_inc(consts, 1)
            pool.memset(PV[:, :].rearrange("p (t w) -> p t w", w=D + 1)[:, :, D:D + 1], -1.0).then_inc(consts, 1)
            pool.memset(half_c[:, :], TANH_SHIFT).then_inc(consts, 1)
            pool.wait_ge(w_in, 16 * WEIGHT_LOADS)

            def phase1(at):
                k = at(0)
                if k.live:
                    pool.wait_ge(x_var, k.n + 1)
                    wait(pool, q_ready, k.n - 1)
                    pool.tensor_tensor(buf(xrstd, k, G), buf(xvar, k, G), pow_c[:, :], ALU.pow).then_inc(x_rstd, 1)
                k = at(1)
                if k.live:
                    pool.wait_ge(q_ready, k.n + 1)
                    pool.tensor_tensor(tiles(chunk(F, k)), tiles(buf(q_c, k)), over_tiles(bd_r),
                                       ALU.add).then_inc(qb_ready, 1)
                    pool.wait_ge(qb_ready, k.n + 1)
                    pool.wait_ge(P_sb, k.n + 1)
                    pool.tensor_tensor(tiles(chunk(F, k)), tiles(chunk(F, k)), pv_chunk(k),
                                       ALU.add).then_inc(pq_ready, 1)

            pool.wait_ge(w_done, 1)
            run_steps(pool, NC, 1, phase1)

            def phase2(at):
                k = at(0)
                if k.live:
                    wait(pool, dT_ps, k.n - 1)
                    pool.tensor_tensor(tiles(buf(diff_c, k)), tiles(chunk(TK, k)),
                                       over_features(per_tile(GAINS[:, T:2 * T], k)), ALU.mult).then_inc(kscaled, 1)
                    pool.wait_ge(kscaled, k.n + 1)
                    pool.tensor_tensor(tiles(buf(diff_c, k)), tiles(buf(diff_c, k)),
                                       over_features(per_tile(SHIFT, k)), ALU.add).then_inc(kpart, 1)
                k = at(4)
                if k.live:
                    pool.wait_ge(fvar_ready, k.n + 1)
                    pool.tensor_tensor(per_tile(RSTDF, k), buf(fvar, k, G), pow_c[:, :], ALU.pow).then_inc(frstd, 1)

            pool.wait_ge(norms, NORM_STEPS)
            pool.wait_ge(tanh_q, NC)
            run_steps(pool, NC, 4, phase2)

            def phase3(at):
                k = at(1)
                if k.live:
                    wait(pool, o_ready, k.n - 1)
                    pool.tensor_tensor(tiles(buf(f2_c, k)), tiles(chunk(F, k)), over_tiles(b2_r),
                                       ALU.add).then_inc(f2_ready, 1)
                k = at(2)
                if k.live:
                    wait(pool, x1_ready, k.n - 1)
                    pool.tensor_tensor(tiles(buf(xb_c, k)), tiles(chunk(X, k)), over_tiles(b_r),
                                       ALU.add).then_inc(xb_ready, 1)
                k = at(4)
                if k.live:
                    if not isinstance(k.n, int) or k.n >= 2:
                        pool.wait_ge(stored[k.buf], 16 * k.pair)
                    pool.wait_ge(x1_ready, k.n + 1)
                    pool.tensor_tensor(tiles(buf(y_c, k)), tiles(buf(x1_c, k)), over_tiles(bf_r),
                                       ALU.add).then_inc(x1b_ready, 1)
                k = at(3)
                if k.live:
                    pool.wait_ge(x1_var, k.n + 1)
                    pool.tensor_tensor(buf(xrstd, k, G), buf(xvar, k, G), pow_c[:, :], ALU.pow).then_inc(x1_rstd, 1)
                k = at(2)
                if k.live:
                    pool.wait_ge(ovar_ready, k.n + 1)
                    pool.tensor_tensor(buf(orstd, k, G), buf(ovar, k, G), pow_c[:, :], ALU.pow).then_inc(orstd_ready, 1)

            run_steps(pool, NC, 4, phase3)

        @block.scalar
        def _(act):
            def phase1(at):
                k = at(0)
                if k.live:
                    act.wait_ge(ctx_sem[k.buf], 16 * (k.pair + 1))
                    act.activation(chunk(TK, k), buf(ctx_c, k), ACT.Tanh).then_inc(tanh_k, 1)
                    act.wait_ge(vT_ps, k.n + 1)
                    wait(act, P_ps, k.n - 1)
                    act.activation(buf(vT_c, k), bank[0][:, :], ACT.Copy).then_inc(vT_sb, 1)
                k = at(1)
                if k.live:
                    act.wait_ge(q_ready, k.n + 1)
                    for i in range(G):
                        last = act.activation(all_tile(TQ, k, i), tile(q_c, k, i), ACT.Tanh,
                                              accum_out=per_tile(SUMQ, k, i, 1))
                    last.then_inc(tanh_q, 1)
                    act.wait_ge(P_ps, k.n + 1)
                    act.activation(pv_chunk(k), tiles(bank[1][:, :]), ACT.Copy).then_inc(P_sb, 1)

            run_steps(act, NC, 1, phase1)

            act.wait_ge(norms, NORM_STEPS)
            act.activation(LRATIO[:, :], NRATIO[:, :], ACT.Ln).then_inc(lratio, 1)

            def phase2(at):
                k = at(3)
                if k.live:
                    act.wait_ge(f_ready, k.n + 1)
                    wait(act, ssf_ready, k.n)
                    for i in range(G):
                        last = act.activation(junk[:, i * D:(i + 1) * D], all_tile(F, k, i), ACT.Square,
                                              accum_out=per_tile(SSF, k, i, 1))
                    last.then_inc(ssf_ready, 1)
                k = at(0)
                if k.live:
                    wait(act, lr_ready, k.n - 1)
                    wait(act, lT_ps, k.n - 1)
                    act.activation(buf(lnq_c, k), chunk(TQ, k), ACT.Ln, bias=half_c[:, 0:1], scale=TANH_GAIN)
                    act.activation(buf(lr_c, k), chunk(TK, k), ACT.Ln, bias=half_c[:, 0:1],
                                   scale=TANH_GAIN).then_inc(ln_ready, 1)
                k = at(1)
                if k.live:
                    wait(act, s_ps, k.n - 1)
                    act.wait_ge(dT_ps, k.n + 1)
                    act.activation(buf(dT_c, k), bank[2][:, :], ACT.Copy).then_inc(dT_sb, 1)
                    act.wait_ge(lT_ps, k.n + 1)
                    act.activation(buf(lT_c, k), bank[3][:, :], ACT.Copy).then_inc(lT_sb, 1)
                k = at(2)
                if k.live:
                    act.wait_ge(s_ps, k.n + 1)
                    wait(act, ep_ps, k.n - 1)
                    for h in range(2):
                        rows_h = slice(h * S, (h + 1) * S)
                        last = act.activation(tiles(buf(E_c, k))[rows_h, :, rows_h],
                                              tiles(bank[4][:, :])[rows_h, :, rows_h],
                                              ACT.Exp, scale=-float(D) ** -0.5)
                    last.then_inc(e_ready, 1)

            act.wait_ge(pq_ready, NC)
            run_steps(act, NC, 3, phase2)

            def phase3(at):
                m, o, h, q = at(1), at(2), at(0), at(5)

                def gelu(j):
                    if m.live:
                        act.wait_ge(m1_ps, HB * m.n + (j + 1))
                        if j == 0:
                            wait(act, m2_ps, m.n - 1)
                        act.activation(buf(hid_c, m, HB * C)[:, j * C:(j + 1) * C], bank[j % 2][:, :], ACT.Gelu,
                                       bias=b1c[:, j:j + 1]).then_inc(gelu_ready, 1)

                gelu(0)
                gelu(1)
                if o.live:
                    act.wait_ge(o_ready, o.n + 1)
                    wait(act, ovar_ready, o.n - 1)
                    wait(act, sso_ready, o.n)
                    for i in range(G):
                        last = act.activation(junk[:, i * D:(i + 1) * D], tile(o_c, o, i), ACT.Square,
                                              accum_out=sso[:, o.buf * G + i:o.buf * G + i + 1])
                    last.then_inc(sso_ready, 1)
                gelu(2)
                gelu(3)
                if h.live:
                    act.wait_ge(hT_ps, h.n + 1)
                    wait(act, m1_ps, HB * (h.n - 1))
                    act.activation(buf(hTh, h), bank[4][:, :], ACT.Copy).then_inc(hi_ready, 1)
                if q.live:
                    act.wait_ge(xqT_ps, q.n + 1)
                    wait(act, ff_ps, q.n - 1)
                    act.activation(buf(xqT_c, q), bank[5][:, :], ACT.Copy).then_inc(xqT_sb, 1)
                    act.wait_ge(ff_ps, q.n + 1)
                    wait(act, y_ready, q.n - 1)
                    act.activation(buf(r16_c, q), bank[6][:, :], ACT.Copy).then_inc(r16_ready, 1)

            act.wait_ge(frstd, FREE_AT)
            run_steps(act, NC, 5, phase3)

        def prep_dve(dve, link):
            for row in (bd_r, b2_r):
                link(dve.tensor_reduce(wq[4][:, 0:1], row, AX.X, ALU.add))
                link(dve.tensor_scalar(wq[4][:, 0:1], wq[4][:, 0:1], 1.0 / D, None, ALU.mult))
                link(dve.tensor_scalar(row, row, wq[4][:, 0:1], None, ALU.subtract))
            link(dve.tensor_scalar(wq[0], Wf_raw, E4M3FN_MAX, -E4M3FN_MAX, ALU.min, ALU.max))
            link(dve.tensor_scalar(wq[1], wq[0], E4M3_SAFE, -E4M3_SAFE, ALU.min, ALU.max))
            link(dve.tensor_copy(raw8[:, 0:D], wq[1], saturate=False))
            link(dve.tensor_copy(wq[1], raw8[:, 0:D]))
            link(dve.tensor_scalar(wq[2], wq[0], 0.5, None, ALU.mult))
            link(dve.tensor_copy(raw8[:, D:2 * D], wq[2], saturate=False))
            link(dve.tensor_scalar(wq[2], raw8[:, D:2 * D], 2.0, None, ALU.mult))
            link(dve.tensor_tensor(wq[0], wq[0], wq[0], ALU.mult))
            link(dve.tensor_scalar(wq[0], wq[0], E4M3_SAFE * E4M3_SAFE, None, ALU.is_gt))
            link(dve.tensor_tensor(wq[2], wq[2], wq[1], ALU.subtract))
            link(dve.tensor_tensor(wq[2], wq[2], wq[0], ALU.mult))
            dve.wait_ge(consts, 5)
            dve.tensor_copy(ident8[:, :], ident[:, :], saturate=False)
            dve.tensor_tensor(wq[1], wq[1], wq[2], ALU.add).then_inc(wfq, 1)
            dve.wait_ge(w_tp, 1)
            link(dve.tensor_reduce(wq[4][:, 0:1], bank[0][:, 0:D], AX.X, ALU.add))
            link(dve.tensor_scalar(wq[4][:, 0:1], wq[4][:, 0:1], 1.0 / D, None, ALU.mult))
            link(dve.tensor_scalar(WdT[:, :], bank[0][:, 0:D], wq[4][:, 0:1], None, ALU.subtract))
            dve.wait_ge(w_tp, 3)
            link(dve.tensor_copy(WfT[:, :], bank[3][:, 0:D]))
            for j in range(HB):
                w2 = bank[2][:, j * D:(j + 1) * D]
                link(dve.tensor_reduce(wq[4][:, 0:1], w2, AX.X, ALU.add))
                link(dve.tensor_scalar(wq[4][:, 0:1], wq[4][:, 0:1], 1.0 / D, None, ALU.mult))
                link(dve.tensor_scalar(W2T[:, j * D:(j + 1) * D], w2, wq[4][:, 0:1], None, ALU.subtract))
            dve.tensor_copy(W1g, bank[1][:, :]).then_inc(w1_sb, 1)
            dve.wait_ge(b1_ps, 1)
            link(dve.tensor_tensor(b1c[:, :], bank[4][:, 0:HB], Wcol[:, 0:HB], ALU.add))
            link(dve.tensor_scalar(W1g, W1g, g_col[:, 0:1], None, ALU.mult))
            link(dve.tensor_copy(W1h[:, :], W1g))
            link(dve.tensor_tensor(W1l[:, :], W1g, W1h[:, :].bitcast(F32), ALU.subtract))
            link(dve.memset(E_c[:, :], 0.0))
            dve.memset(sso[:, :], 0.0).then_inc(w_done, 1)

        @block.vector
        def _(dve):
            steps = [0]

            def link(ins):
                steps[0] += 1
                ins.then_inc(wv, 1)
                dve.wait_ge(wv, steps[0])

            dve.wait_ge(w_in, 16 * WEIGHT_LOADS)
            prep_dve(dve, link)

            def mean_and_var(k, taken, halves, terms, done):
                st = xstat[:, k.buf * G * 6:(k.buf + 1) * G * 6].rearrange("p (t s) -> p t s", s=6)
                mv = xmv[:, k.buf * G * 2:(k.buf + 1) * G * 2].rearrange("p (t s) -> p t s", s=2)
                gap = buf(xgap, k, G)
                dve.wait_ge(taken, k.n + 1)
                dve.tensor_tensor(mv, st[:, :, 1:3], st[:, :, 4:6], ALU.add)
                dve.tensor_tensor(gap, st[:, :, 1], st[:, :, 4], ALU.subtract).then_inc(halves, 1)
                dve.wait_ge(halves, k.n + 1)
                dve.scalar_tensor_tensor(out=gap, in0=gap, scalar=0.25, in1=gap, op0=ALU.mult, op1=ALU.mult)
                dve.tensor_scalar(mv[:, :, 1], mv[:, :, 1], 1.0 / D, LN_EPS, ALU.mult, ALU.add)
                dve.tensor_scalar(mv[:, :, 0], mv[:, :, 0], 0.5, None, ALU.mult).then_inc(terms, 1)
                dve.wait_ge(terms, k.n + 1)
                dve.tensor_tensor(buf(xvar, k, G), gap, mv[:, :, 1], ALU.add).then_inc(done, 1)

            def phase1(at):
                k = at(0)
                if k.live:
                    dve.wait_ge(x_in[k.buf], 16 * (k.pair + 1))
                    for i in range(G):
                        last = dve.bn_stats(xstat[:, (k.buf * G + i) * 6:(k.buf * G + i + 1) * 6], all_tile(X, k, i))
                    last.then_inc(x_bn, 1)
                    mean_and_var(k, x_bn, x_halves, x_terms, x_var)
                k = at(1)
                if k.live:
                    dve.wait_ge(x_rstd, k.n + 1)
                    wait(dve, tanh_q, k.n - 1)
                    wait(dve, qb_ready, k.n - 1)
                    for i in range(G):
                        m = (k.buf * G + i) * 2
                        last = dve.tensor_scalar(tile(q_c, k, i), all_tile(X, k, i), xmv[:, m:m + 1],
                                                 xrstd[:, k.buf * G + i:k.buf * G + i + 1], ALU.subtract, ALU.mult)
                    last.then_inc(q_ready, 1)
                    dve.wait_ge(tanh_k, k.n + 1)
                    dve.tensor_reduce(per_tile(SUMK, k), tiles(chunk(TK, k)), AX.X, ALU.add).then_inc(ksum, 1)

            run_steps(dve, NC, 1, phase1)

            n = [0]

            def norm(ins):
                n[0] += 1
                ins.then_inc(norms, 1)
                dve.wait_ge(norms, n[0])

            dve.wait_ge(ksum, NC)
            dve.wait_ge(tanh_q, NC)
            norm(dve.tensor_scalar(NORM[:, :], SUM[:, :], TANH_GAIN, TANH_SHIFT * D, ALU.mult, ALU.add))
            norm(dve.tensor_scalar(NORM[:, :], NORM[:, :], PROB_EPS, None, ALU.add))
            norm(dve.reciprocal(RNORM[:, :], NORM[:, :]))
            norm(dve.tensor_scalar(GAINS[:, 0:T], RNORM[:, 0:T], TANH_GAIN, None, ALU.mult))
            dve.tensor_scalar(GAINS[:, T:2 * T], RNORM[:, T:2 * T], -TANH_GAIN, None, ALU.mult)
            norm(dve.tensor_tensor(SHIFT[:, :], RNORM[:, 0:T], RNORM[:, T:2 * T], ALU.subtract))
            norm(dve.tensor_scalar(SHIFT[:, :], SHIFT[:, :], TANH_SHIFT, None, ALU.mult))
            norm(dve.tensor_tensor(NRATIO[:, :], NORM[:, T:2 * T], RNORM[:, 0:T], ALU.mult))
            assert n[0] == NORM_STEPS

            def phase2(at):
                k = at(0)
                if k.live:
                    dve.wait_ge(kpart, k.n + 1)
                    for i in range(G):
                        last = dve.scalar_tensor_tensor(out=tile(diff_c, k, i), in0=all_tile(TQ, k, i),
                                                        scalar=per_tile(GAINS[:, 0:T], k, i, 1),
                                                        in1=tile(diff_c, k, i), op0=ALU.mult, op1=ALU.add)
                    last.then_inc(diff_ready, 1)
                    dve.wait_ge(ln_ready, k.n + 1)
                    for i in range(G):
                        last = dve.scalar_tensor_tensor(out=tile(lr_c, k, i), in0=tile(lnq_c, k, i),
                                                        scalar=per_tile(LRATIO, k, i, 1), in1=tile(lr_c, k, i),
                                                        op0=ALU.add, op1=ALU.subtract)
                    last.then_inc(lr_ready, 1)
                k = at(2)
                if k.live:
                    dve.wait_ge(ep_ps, k.n + 1)
                    for hb in range(2):
                        o = k.buf * G + 2 * hb
                        last = dve.reciprocal(nrden[:, o:o + 2],
                                              bank[5 + hb][:, :].rearrange("p (t w) -> p t w", w=EPW)[:, :, D])
                    last.then_inc(rden, 1)
                    dve.wait_ge(rden, k.n + 1)
                    for i in range(G):
                        ep = bank[5 + i // 2][:, (i % 2) * EPW:(i % 2) * EPW + D]
                        last = dve.scalar_tensor_tensor(out=all_tile(F, k, i), in0=ep,
                                                        scalar=nrden[:, k.buf * G + i:k.buf * G + i + 1],
                                                        in1=all_tile(F, k, i), op0=ALU.mult, op1=ALU.add)
                    last.then_inc(f_ready, 1)
                k = at(3)
                if k.live:
                    dve.wait_ge(ssf_ready, k.n + 1)
                    wait(dve, frstd, k.n - 1)
                    dve.tensor_scalar(buf(fvar, k, G), per_tile(SSF, k), 1.0 / D, LN_EPS,
                                      ALU.mult, ALU.add).then_inc(fvar_ready, 1)

            dve.wait_ge(lratio, 1)
            dve.wait_ge(pq_ready, NC)
            run_steps(dve, NC, 3, phase2)

            def phase3(at):
                k = at(2)
                if k.live:
                    dve.wait_ge(m2_ps, k.n + 1)
                    dve.wait_ge(f2_ready, k.n + 1)
                    wait(dve, sso_ready, k.n - 1)
                    dve.tensor_tensor(buf(o_c, k), bank[2 + k.buf][:, :], buf(f2_c, k), ALU.add).then_inc(o_ready, 1)
                k = at(0)
                if k.live:
                    wait(dve, hT_ps, k.n - 1)
                    dve.wait_ge(frstd, k.n + 1)
                    dve.tensor_tensor(tiles(buf(h_c, k)), tiles(chunk(F, k)), over_features(per_tile(RSTDF, k)),
                                      ALU.mult).then_inc(h_ready, 1)
                k = at(3)
                if k.live:
                    dve.wait_ge(orstd_ready, k.n + 1)
                    wait(dve, x1b_ready, k.n - 1)
                    wait(dve, xq_ready, k.n - 1)
                    for i in range(G):
                        last = dve.scalar_tensor_tensor(out=tile(x1_c, k, i), in0=tile(o_c, k, i),
                                                        scalar=orstd[:, k.buf * G + i:k.buf * G + i + 1],
                                                        in1=g_r, op0=ALU.mult, op1=ALU.mult)
                    last.then_inc(xn_ready, 1)
                    dve.wait_ge(xn_ready, k.n + 1)
                    dve.wait_ge(xb_ready, k.n + 1)
                    dve.tensor_tensor(buf(x1_c, k), buf(x1_c, k), buf(xb_c, k), ALU.add).then_inc(x1_ready, 1)
                    dve.wait_ge(x1_ready, k.n + 1)
                    for i in range(G):
                        at_i = k.buf * G + i
                        last = dve.bn_stats(xstat[:, at_i * 6:at_i * 6 + 6], tile(x1_c, k, i))
                    last.then_inc(x1_bn, 1)
                    wait(dve, x1_rstd, k.n - 1)
                    mean_and_var(k, x1_bn, x1_halves, x1_terms, x1_var)
                k = at(4)
                if k.live:
                    wait(dve, xqT_ps, k.n - 1)
                    dve.wait_ge(x1_rstd, k.n + 1)
                k = at(2)
                if k.live:
                    dve.wait_ge(sso_ready, k.n + 1)
                    wait(dve, orstd_ready, k.n - 1)
                    dve.tensor_scalar(buf(ovar, k, G), buf(sso, k, G), 1.0 / D, LN_EPS,
                                      ALU.mult, ALU.add).then_inc(ovar_ready, 1)
                k = at(4)
                if k.live:
                    for i in range(G):
                        m = (k.buf * G + i) * 2
                        last = dve.tensor_scalar(tile(xq_c, k, i), tile(x1_c, k, i), xmv[:, m:m + 1],
                                                 xrstd[:, k.buf * G + i:k.buf * G + i + 1],
                                                 ALU.subtract, ALU.mult, saturate=False)
                    last.then_inc(xq_ready, 1)
                k = at(0)
                if k.live:
                    dve.wait_ge(hi_ready, k.n + 1)
                    dve.tensor_tensor(buf(hTl, k), bank[4][:, :], buf(hTh, k).bitcast(F32),
                                      ALU.subtract).then_inc(lo_ready, 1)
                k = at(5)
                if k.live:
                    dve.wait_ge(r16_ready, k.n + 1)
                    dve.wait_ge(x1b_ready, k.n + 1)
                    dve.tensor_tensor(buf(y_c, k), buf(r16_c, k), buf(y_c, k), ALU.add).then_inc(y_ready, 1)

            run_steps(dve, NC, 5, phase3)

        @block.tensor
        def _(pe):
            pe.wait_ge(consts, 5)
            pe.wait_ge(w_in, 16 * WEIGHT_LOADS)
            pe.transpose(bank[0][:, 0:D], Wd_raw, ident[:, :]).then_inc(w_tp, 1)
            for j in range(HB):
                last = pe.transpose(bank[1][:, j * D:(j + 1) * D], W1_raw[:, j * D:(j + 1) * D], ident[:, :])
                last = pe.transpose(bank[2][:, j * D:(j + 1) * D], W2_raw[:, j * D:(j + 1) * D], ident[:, :])
            last.then_inc(w_tp, 1)
            pe.wait_ge(wfq, 1)
            pe.transpose(bank[3][:, 0:D], wq[1], ident[:, :]).then_inc(w_tp, 1)
            pe.wait_ge(w1_sb, 1)
            for j in range(HB):
                last = pe.matmul(bank[4][:, j:j + 1], W1g[:, j * D:(j + 1) * D], b_col[:, :], start=True, stop=True)
            last.then_inc(b1_ps, 1)
            pe.wait_ge(w_done, 1)

            def phase1(at):
                k = at(0)
                if k.live:
                    pe.wait_ge(ctx_sem[k.buf], 16 * (k.pair + 1))
                    wait(pe, vT_sb, k.n)
                    for i in range(G):
                        last = pe.transpose(bank[0][:, i * D:(i + 1) * D], tile(ctx_c, k, i), ident[:, :])
                    last.then_inc(vT_ps, 1)
                    pe.wait_ge(vT_sb, k.n + 1)
                    wait(pe, P_sb, k.n)
                    for i in range(G):
                        last = pe.matmul(bank[1][:, i * D:(i + 1) * D], tile(vT_c, k, i), WdT[:, :],
                                         start=True, stop=True)
                    last.then_inc(P_ps, 1)

            run_steps(pe, NC, 0, phase1)

            def phase2(at):
                k = at(0)
                if k.live:
                    pe.wait_ge(diff_ready, k.n + 1)
                    wait(pe, dT_sb, k.n)
                    for i in range(G):
                        last = pe.transpose(bank[2][:, i * D:(i + 1) * D], tile(diff_c, k, i), ident[:, :])
                    last.then_inc(dT_ps, 1)
                    pe.wait_ge(lr_ready, k.n + 1)
                    wait(pe, lT_sb, k.n)
                    for i in range(G):
                        last = pe.transpose(bank[3][:, i * D:(i + 1) * D], tile(lr_c, k, i), ident[:, :])
                    last.then_inc(lT_ps, 1)
                k = at(1)
                if k.live:
                    pe.wait_ge(dT_sb, k.n + 1)
                    pe.wait_ge(lT_sb, k.n + 1)
                    wait(pe, e_ready, k.n)
                    for i in range(G):
                        last = pe.matmul(bank[4][:, i * D:(i + 1) * D], tile(lT_c, k, i), tile(dT_c, k, i),
                                         start=True, stop=True)
                    last.then_inc(s_ps, 1)
                k = at(2)
                if k.live:
                    pe.wait_ge(e_ready, k.n + 1)
                    wait(pe, f_ready, k.n)
                    for i in range(G):
                        o = (i % 2) * EPW
                        last = pe.matmul(bank[5 + i // 2][:, o:o + D + 1], tile(E_c, k, i),
                                         all_tile(PV, k, i, D + 1, D + 1), start=True, stop=True)
                    last.then_inc(ep_ps, 1)

            pe.wait_ge(P_sb, NC)
            run_steps(pe, NC, 2, phase2)

            def phase3(at):
                h, m, q = at(0), at(1), at(5)

                def mlp1(j):
                    if m.live:
                        if j == 0:
                            pe.wait_ge(hi_ready, m.n + 1)
                            pe.wait_ge(lo_ready, m.n + 1)
                        wait(pe, gelu_ready, HB * m.n + (j - 1))
                        ps = bank[j % 2][:, :]
                        w_hi, w_lo = W1h[:, j * P:(j + 1) * P], W1l[:, j * P:(j + 1) * P]
                        pe.matmul(ps, w_hi, buf(hTh, m), start=True, stop=False)
                        pe.matmul(ps, w_hi, buf(hTl, m), start=False, stop=False)
                        pe.matmul(ps, w_lo, buf(hTh, m), start=False, stop=True).then_inc(m1_ps, 1)

                def mlp2(j):
                    if m.live:
                        pe.wait_ge(gelu_ready, HB * m.n + (j + 1))
                        if j == 0:
                            wait(pe, o_ready, m.n - 1)
                        for i in range(G):
                            last = pe.matmul(bank[2 + m.buf][:, i * D:(i + 1) * D],
                                             buf(hid_c, m, HB * C)[:, j * C + i * D:j * C + (i + 1) * D],
                                             W2T[:, j * D:(j + 1) * D], start=(j == 0 and i == 0),
                                             stop=(j == HB - 1), skip_group_check=True)
                        if j == HB - 1:
                            last.then_inc(m2_ps, 1)

                mlp1(0)
                mlp1(1)
                mlp2(0)
                mlp1(2)
                mlp2(1)
                mlp1(3)
                if q.live:
                    pe.wait_ge(xq_ready, q.n + 1)
                    wait(pe, xqT_sb, q.n)
                if h.live:
                    pe.wait_ge(h_ready, h.n + 1)
                    wait(pe, lo_ready, h.n)
                    wait(pe, hi_ready, h.n)
                    for i in range(G):
                        last = pe.transpose(bank[4][:, i * D:(i + 1) * D], tile(h_c, h, i), ident[:, :])
                    last.then_inc(hT_ps, 1)
                if q.live:
                    for i in range(G):
                        last = pe.matmul(bank[5][:, i * D:(i + 1) * D], tile(xq_c, q, i), ident8[:, :],
                                         start=True, stop=True)
                    last.then_inc(xqT_ps, 1)
                mlp2(2)
                mlp2(3)
                if q.live:
                    pe.wait_ge(xqT_sb, q.n + 1)
                    wait(pe, r16_ready, q.n)
                    for i in range(G):
                        last = pe.matmul(bank[6][:, i * D:(i + 1) * D], tile(xqT_c, q, i), WfT[:, :],
                                         start=True, stop=True)
                    last.then_inc(ff_ps, 1)

            pe.wait_ge(f_ready, NC)
            run_steps(pe, NC, 5, phase3)


_INS = ['x', 'ctx_1024', 'L0_xattn_W_diff', 'L0_xattn_b_diff', 'L0_xattn_ln_g', 'L0_xattn_ln_b', 'L0_xattn_W1',
        'L0_xattn_b1', 'L0_xattn_W2', 'L0_xattn_b2', 'L0_ffn_weight', 'L0_ffn_bias']


def kernel(**inputs):
    import numpy as _np
    import concourse.bacc as _bacc
    from concourse import mybir as _mybir
    from concourse.bass_utils import run_bass_kernel_spmd as _run

    nc = _bacc.Bacc("TRN2", target_bir_lowering=False, num_devices=1)
    arrays, args = {}, []
    for name in _INS:
        a = _np.ascontiguousarray(inputs[name])
        arrays[f"in_{name}_dram"] = a
        args.append(nc.dram_tensor(f"in_{name}_dram", a.shape, _mybir.dt.from_np(a.dtype), kind="ExternalInput").ap())
    shape = arrays["in_x_dram"].shape
    args.append(nc.dram_tensor("out_0_dram", shape, _mybir.dt.float32, kind="ExternalOutput").ap())
    xattn_ffn_kernel(nc, *args)
    r = _run(nc, [arrays], core_ids=[0])
    return r.results[0]["out_0_dram"]
```

```python
from contextlib import ExitStack

import concourse.bass as bass
from concourse import mybir

F32 = mybir.dt.float32
F32R = mybir.dt.float32r
BF16 = mybir.dt.bfloat16
F16 = mybir.dt.float16
F8 = mybir.dt.float8e4
ALU = mybir.AluOpType
ACT = mybir.ActivationFunctionType
AX = mybir.AxisListType

P = 128
LN_EPS = 1e-5
PROB_EPS = 1e-8
TANH_GAIN, TANH_SHIFT = 0.499, 0.5
E4M3FN_MAX = 448.0
E4M3_SAFE = 128.0


class Chunk:

    def __init__(self, half, odd, lag, chunks):
        self.n = 2 * half + (odd - lag)
        self.pair = half + (odd - lag) // 2
        self.buf = (odd - lag) % 2
        self.live = not isinstance(half, int) or 0 <= self.n < chunks


def wait(eng, sem, count):
    if isinstance(count, int) and count <= 0:
        return
    eng.wait_ge(sem, count)


def is_chunk(k, n):
    return isinstance(k.n, int) and k.n == n


def run_steps(eng, chunks, last_lag, step):
    first = (last_lag + 3) // 2
    for n in range(2 * first):
        step(lambda lag, n=n: Chunk(n // 2, n % 2, lag, chunks))
    with eng.Fori(first, chunks // 2) as half:
        for odd in range(2):
            step(lambda lag, odd=odd: Chunk(half, odd, lag, chunks))
    for n in range(chunks, chunks + last_lag):
        step(lambda lag, n=n: Chunk(n // 2, n % 2, lag, chunks))


def xattn_ffn_kernel(nc, x, ctx_in, W_diff, b_diff, ln_g, ln_b, W1, b1, W2, b2, Wf, bf, out):
    B, S, D = x.shape
    HID = W1.shape[0]
    HB = HID // P
    assert D == P and 2 * S == P
    T = B * S // P
    G = 4
    C = G * D
    NC = T // G
    EPW = 256

    x_d = x.rearrange("b s d -> (b s) d").rearrange("(c t p) d -> c p t d", t=G, p=P)
    ctx_d = ctx_in.rearrange("b s d -> (b s) d").rearrange("(c t p) d -> c p t d", t=G, p=P)
    out_d = out.rearrange("b s d -> (b s) d").rearrange("(c t p) d -> c p t d", t=G, p=P)

    with ExitStack() as ctx:
        def sb(name, shape, dt=F32):
            return ctx.enter_context(nc.sbuf_tensor(name, shape, dt))

        def sem(name):
            return ctx.enter_context(nc.semaphore(name))

        bank = [ctx.enter_context(nc.psum_tensor(f"bank{i}", [P, 512], F32)) for i in range(8)]

        X = sb("X", [P, T * D])
        TQ = sb("TQ", [P, T * D])
        TK = sb("TK", [P, T * D])
        F = sb("F", [P, T * D])
        PV = sb("PV", [P, T * (D + 1)])
        SUM = sb("SUM", [P, 2 * T])
        SUMQ, SUMK = SUM[:, 0:T], SUM[:, T:2 * T]
        NORM = sb("NORM", [P, 2 * T])
        RNORM = sb("RNORM", [P, 2 * T])
        GAINS = sb("GAINS", [P, 2 * T])
        SHIFT = sb("SHIFT", [P, T])
        NRATIO = sb("NRATIO", [P, T])
        LRATIO = sb("LRATIO", [P, T])
        VARF = sb("VARF", [P, T])
        RSTDF = sb("RSTDF", [P, T])

        ident = sb("ident", [P, P])
        half_c = sb("half_c", [P, 1])
        pow_c = sb("pow_c", [P, G])
        eps_c = sb("eps_c", [P, G])
        WdT = sb("WdT", [P, D])
        W1h = sb("W1h", [P, HID], F32R)
        W1l = sb("W1l", [P, HID], F32R)
        b1c = sb("b1c", [P, HB])
        b1_raw = sb("b1_raw", [P, HB])
        W2T = sb("W2T", [P, HB * D])
        Wf_raw = sb("Wf_raw", [P, D])
        Wf8 = sb("Wf8", [P, D], F8)
        WfT = sb("WfT", [P, D], BF16)
        ident8 = sb("ident8", [P, P], F8)
        rows = sb("rows", [P, 5 * D])
        bd_r, b2_r, g_r, b_r, bf_r = (rows[:, i * D:(i + 1) * D] for i in range(5))
        row_mean = sb("row_mean", [P, 1])
        g_col = sb("g_col", [P, 1])
        b_col = sb("b_col", [P, 1])

        ctx_c = sb("ctx_c", [P, 2 * C])
        q_c = sb("q_c", [P, 2 * C])
        vT_c = sb("vT_c", [P, 2 * C])
        lnq_c, diff_c, dT_c = ctx_c, q_c, vT_c
        lr_c = sb("lr_c", [P, 2 * C])
        lT_c = sb("lT_c", [P, 2 * C])
        E_c = sb("E_c", [P, 2 * C])
        hTh = sb("hTh", [P, 2 * C], F32R)
        hTl = sb("hTl", [P, 2 * C], F32R)
        xstat = sb("xstat", [P, 2 * G * 6])
        xmv = sb("xmv", [P, 2 * G * 2])
        xgap = sb("xgap", [P, 2 * G])
        xvar = sb("xvar", [P, 2 * G])
        xrstd = sb("xrstd", [P, 2 * G])
        nrden = sb("nrden", [P, 2 * G])
        sso = sb("sso", [P, 2 * G])
        ovar = sb("ovar", [P, 2 * G])
        orstd = sb("orstd", [P, 2 * G])

        hid_c = TQ[:, 0:2 * HB * C]
        h_c = q_c
        x1_c = vT_c
        xq_c = ctx_c[:, 0:C // 2].bitcast(F8)
        xqT_c = ctx_c[:, C:2 * C].bitcast(BF16)
        r16_c = lr_c[:, 0:C].bitcast(F16)

        Wd_raw = E_c[:, 0:D]
        W1_raw, W1u = lr_c[:, 0:HB * D], lr_c[:, C:C + HID]
        W2_raw, W1g = lT_c[:, 0:HID], lT_c[:, C:C + HID]
        wq = [SUM[:, :], NORM[:, :], RNORM[:, :]]
        centre = E_c[:, D:2 * D]
        VT_B, P_B = (bank[0], bank[7]), (bank[1], bank[2])
        D_B, L_B, S_B, EP_B = bank[2], bank[3], (bank[4], bank[7]), ((bank[5], bank[6]), (bank[0], bank[1]))
        M1_B, M2_B, HT_B, XQ_B, FF_B = (bank[0], bank[1]), (bank[2], bank[3]), bank[4], bank[5], bank[6]

        def chunk(t, k, width=C):
            return t[:, bass.ds(k.n * width, width)] if not isinstance(k.n, int) else t[:, k.n * width:(k.n + 1) * width]

        def buf(t, k, width=C):
            return t[:, k.buf * width:(k.buf + 1) * width]

        def tile(t, k, i):
            return t[:, k.buf * C + i * D:k.buf * C + (i + 1) * D]

        def tiles(ap):
            return ap.rearrange("p (t d) -> p t d", d=D)

        def per_tile(t, k, i=0, n=G):
            at = k.n * G + i
            return t[:, bass.ds(at, n)] if not isinstance(at, int) else t[:, at:at + n]

        def all_tile(t, k, i, width=D, stride=D):
            at = (k.n * G + i) * stride
            return t[:, bass.ds(at, width)] if not isinstance(at, int) else t[:, at:at + width]

        def over_tiles(row):
            return row.unsqueeze(1).broadcast_to([P, G, D])

        def over_features(col):
            return col.unsqueeze(2).broadcast_to([P, G, D])

        def pv_chunk(k):
            w = D + 1
            at = k.n * G * w
            ap = PV[:, bass.ds(at, G * w)] if not isinstance(at, int) else PV[:, at:at + G * w]
            return ap.rearrange("p (t w) -> p t w", w=w)[:, :, 0:D]

        wd_in, bd_in, bd_ready, rows_in, w_in, wf_in, consts = sem("wd_in"), sem("bd_in"), sem("bd_ready"), sem("rows_in"), sem("w_in"), sem("wf_in"), sem("consts")
        rows_ready, wd_ps, wd_sb, w_ps, w_sb = (
            sem("rows_ready"), sem("wd_ps"), sem("wd_sb"), sem("w_ps"), sem("w_sb"))
        b1_ps, w_done, wf_step, wf_q, wf_ps, wf_sb, fb_ready, e_zero = (
            sem("b1_ps"), sem("w_done"), sem("wf_step"), sem("wf_q"), sem("wf_ps"), sem("wf_sb"),
            sem("fb_ready"), sem("e_zero"))
        x_in = [sem(f"x_in{i}") for i in range(2)]
        ctx_sem = [sem(f"ctx_in{i}") for i in range(2)]
        x_bn, x_halves, x_terms = sem("x_bn"), sem("x_halves"), sem("x_terms")
        x_var, x_rstd, xb_ready = sem("x_var"), sem("x_rstd"), sem("xb_ready")
        q_ready, qb_ready, pq_ready = sem("q_ready"), sem("qb_ready"), sem("pq_ready")
        tanh_k, tanh_q = sem("tanh_k"), sem("tanh_q")
        vT_ps, vT_sb, P_ps, P_sb = sem("vT_ps"), sem("vT_sb"), sem("P_ps"), sem("P_sb")
        norms, lratio = sem("norms"), sem("lratio")
        kscaled = sem("kscaled")
        kpart, ln_ready, diff_ready, lr_ready = sem("kpart"), sem("ln_ready"), sem("diff_ready"), sem("lr_ready")
        dT_ps, dT_sb, lT_ps, lT_sb = sem("dT_ps"), sem("dT_sb"), sem("lT_ps"), sem("lT_sb")
        s_ps, e_ready, ep_ps, rden, f_ready = sem("s_ps"), sem("e_ready"), sem("ep_ps"), sem("rden"), sem("f_ready")
        fvar_ready = sem("fvar_ready")
        h_ready, hT_ps, hi_ready, lo_ready = sem("h_ready"), sem("hT_ps"), sem("hi_ready"), sem("lo_ready")
        m1_ps, gelu_ready, m2_ps, o_ready = sem("m1_ps"), sem("gelu_ready"), sem("m2_ps"), sem("o_ready")
        fln_ready, frstd, ovar_ready, oeps_ready, orstd_ready = (
            sem("fln_ready"), sem("frstd"), sem("ovar_ready"), sem("oeps_ready"), sem("orstd_ready"))
        xn_ready, x1_ready, x1_bn, x1_halves, x1_terms, x1_var, x1_rstd = (
            sem("xn_ready"), sem("x1_ready"), sem("x1_bn"), sem("x1_halves"), sem("x1_terms"), sem("x1_var"),
            sem("x1_rstd"))
        x1b_ready, xq_ready, xqT_ps, xqT_sb, ff_ps, r16_ready, y_ready = (
            sem("x1b_ready"), sem("xq_ready"), sem("xqT_ps"), sem("xqT_sb"), sem("ff_ps"), sem("r16_ready"),
            sem("y_ready"))
        stored = sem("stored")

        row_step = sem("row_step")
        CONSTS = 8
        NORM_STEPS = 4
        block = ctx.enter_context(nc.Block())

        @block.sync
        def _(sp):
            def load(k):
                wait(sp, x_var, k.n - 1)
                sp.dma_start(tiles(chunk(X, k)), x_d[k.n]).then_inc(x_in[k.buf], 16)
                wait(sp, tanh_k, k.n - 1)
                wait(sp, vT_ps, k.n - 1)
                sp.dma_start(tiles(buf(ctx_c, k)), ctx_d[k.n]).then_inc(ctx_sem[k.buf], 16)

            for n in range(2):
                load(Chunk(0, n, 0, NC))
            for row, vec in ((b2_r, b2), (g_r, ln_g), (b_r, ln_b), (bf_r, bf)):
                sp.dma_start(row, vec.unsqueeze(0).broadcast_to([P, D])).then_inc(rows_in, 16)
            sp.dma_start(W1_raw.rearrange("p (j d) -> p j d", d=D),
                         W1.rearrange("(j p) d -> p j d", p=P)).then_inc(w_in, 16)
            sp.dma_start(W2_raw, W2).then_inc(w_in, 16)
            sp.dma_start(g_col[:, :], ln_g.unsqueeze(1), allow_slow_non_contiguous=True).then_inc(w_in, 16)
            sp.dma_start(b_col[:, :], ln_b.unsqueeze(1), allow_slow_non_contiguous=True).then_inc(w_in, 16)
            sp.dma_start(b1_raw[:, :], b1.rearrange("(j p) -> p j", p=P),
                         allow_slow_non_contiguous=True).then_inc(w_in, 16)
            sp.dma_start(Wf_raw[:, :], Wf).then_inc(wf_in, 16)
            with sp.Fori(1, NC // 2) as half:
                for odd in range(2):
                    load(Chunk(half, odd, 0, NC))

            def store(k):
                wait(sp, y_ready, k.n + 1)
                sp.dma_start(out_d[k.n], tiles(chunk(F, k))).then_inc(stored, 16)

            with sp.Fori(0, NC // 2) as half:
                for odd in range(2):
                    store(Chunk(half, odd, 0, NC))
            sp.wait_ge(stored, 16 * NC)

        @block.gpsimd
        def _(pool):
            pool.memset(ident[:, :], 0.0).then_inc(consts, 1)
            pool.wait_ge(consts, 1)
            pool.affine_select(out=ident[:, :], in_=ident[:, :], compare_op=ALU.not_equal, fill=1.0,
                               base=0, pattern=[[-1, P]], channel_multiplier=1).then_inc(consts, 1)
            pool.memset(pow_c[:, :], -0.5).then_inc(consts, 1)
            pool.wait_ge(consts, 3)
            pool.tensor_scalar(centre, ident[:, :], -1.0 / D, None, ALU.add).then_inc(consts, 1)
            pool.memset(eps_c[:, :], LN_EPS).then_inc(consts, 1)
            pool.memset(half_c[:, :], TANH_SHIFT).then_inc(consts, 1)
            pool.memset(PV[:, :].rearrange("p (t w) -> p t w", w=D + 1)[:, :, D:D + 1], -1.0).then_inc(consts, 1)

            def phase1(at):
                k = at(0)
                if k.live:
                    pool.wait_ge(x_var, k.n + 1)
                    wait(pool, q_ready, k.n - 1)
                    pool.tensor_tensor(buf(xrstd, k, G), buf(xvar, k, G), pow_c[:, :], ALU.pow).then_inc(x_rstd, 1)
                k = at(1)
                if k.live:
                    pool.wait_ge(q_ready, k.n + 1)
                    pool.tensor_tensor(tiles(chunk(F, k)), tiles(buf(q_c, k)), over_tiles(bd_r),
                                       ALU.add).then_inc(qb_ready, 1)

            pool.wait_ge(bd_ready, 1)
            run_steps(pool, NC, 1, phase1)

            pool.tensor_copy(ident8[:, :], ident[:, :], saturate=False).then_inc(consts, 1)
            pool.wait_ge(w_ps, 1)
            pool.memset(E_c[:, :], 0.0).then_inc(e_zero, 1)

            def phase2(at):
                k = at(0)
                if k.live:
                    wait(pool, dT_ps, k.n - 1)
                    pool.tensor_tensor(tiles(buf(diff_c, k)), tiles(chunk(TK, k)),
                                       over_features(per_tile(GAINS[:, T:2 * T], k)), ALU.mult).then_inc(kscaled, 1)
                    pool.wait_ge(kscaled, k.n + 1)
                    pool.tensor_tensor(tiles(buf(diff_c, k)), tiles(buf(diff_c, k)),
                                       over_features(per_tile(SHIFT, k)), ALU.add).then_inc(kpart, 1)
                    pool.tensor_tensor(tiles(chunk(X, k)), tiles(chunk(X, k)), over_tiles(b_r),
                                       ALU.add).then_inc(xb_ready, 1)

            pool.wait_ge(norms, NORM_STEPS)
            pool.wait_ge(tanh_k, NC)
            pool.wait_ge(tanh_q, NC)
            run_steps(pool, NC, 0, phase2)

            n = [0]

            def link(ins):
                n[0] += 1
                ins.then_inc(wf_step, 1)
                pool.wait_ge(wf_step, n[0])

            pool.wait_ge(wf_in, 16)
            link(pool.tensor_scalar(wq[0], Wf_raw[:, :], E4M3FN_MAX, -E4M3FN_MAX, ALU.min, ALU.max))
            link(pool.tensor_scalar(wq[1], wq[0], E4M3_SAFE, -E4M3_SAFE, ALU.min, ALU.max))
            link(pool.tensor_copy(Wf8[:, :], wq[1], saturate=False))
            link(pool.tensor_copy(wq[1], Wf8[:, :]))
            link(pool.tensor_scalar(wq[2], wq[0], 0.5, None, ALU.mult))
            link(pool.tensor_copy(Wf8[:, :], wq[2], saturate=False))
            link(pool.tensor_copy(wq[2], Wf8[:, :]))
            link(pool.tensor_scalar(wq[2], wq[2], 2.0, None, ALU.mult))
            link(pool.tensor_tensor(wq[0], wq[0], wq[0], ALU.mult))
            link(pool.tensor_scalar(wq[0], wq[0], E4M3_SAFE * E4M3_SAFE, None, ALU.is_gt))
            link(pool.tensor_tensor(wq[2], wq[2], wq[1], ALU.subtract))
            link(pool.tensor_tensor(wq[2], wq[2], wq[0], ALU.mult))
            pool.tensor_tensor(wq[1], wq[1], wq[2], ALU.add).then_inc(wf_q, 1)

            def phase3(at):
                k = at(6)
                if k.live:
                    pool.wait_ge(r16_ready, k.n + 1)
                    pool.wait_ge(x1b_ready, k.n + 1)
                    pool.tensor_tensor(chunk(F, k), buf(r16_c, k), chunk(F, k), ALU.add).then_inc(y_ready, 1)
                k = at(4)
                if k.live:
                    pool.wait_ge(x1_ready, k.n + 1)
                    pool.tensor_tensor(tiles(chunk(F, k)), tiles(buf(x1_c, k)), over_tiles(bf_r),
                                       ALU.add).then_inc(x1b_ready, 1)
                k = at(0)
                if k.live:
                    pool.wait_ge(h_ready, k.n + 1)
                    pool.tensor_tensor(tiles(chunk(F, k)), tiles(chunk(F, k)), over_tiles(b2_r),
                                       ALU.add).then_inc(fb_ready, 1)
                k = at(2)
                if k.live:
                    pool.wait_ge(ovar_ready, k.n + 1)
                    wait(pool, xn_ready, k.n - 1)
                    pool.tensor_tensor(buf(ovar, k, G), buf(sso, k, G), eps_c[:, :], ALU.add).then_inc(oeps_ready, 1)
                    pool.wait_ge(oeps_ready, k.n + 1)
                    pool.tensor_tensor(buf(orstd, k, G), buf(ovar, k, G), pow_c[:, :], ALU.pow).then_inc(orstd_ready, 1)
                k = at(3)
                if k.live:
                    pool.wait_ge(x1_var, k.n + 1)
                    wait(pool, xq_ready, k.n - 1)
                    pool.tensor_tensor(buf(xrstd, k, G), buf(xvar, k, G), pow_c[:, :], ALU.pow).then_inc(x1_rstd, 1)

            pool.wait_ge(rows_ready, 1)
            run_steps(pool, NC, 6, phase3)

        @block.scalar
        def _(act):
            act.dma_start(Wd_raw, W_diff).then_inc(wd_in, 16)
            act.dma_start(bd_r, b_diff.unsqueeze(0).broadcast_to([P, D])).then_inc(bd_in, 16)
            act.wait_ge(wd_ps, 1)
            act.activation(WdT[:, :], bank[6][:, 0:D], ACT.Copy).then_inc(wd_sb, 1)

            def phase1(at):
                k = at(0)
                if k.live:
                    act.wait_ge(ctx_sem[k.buf], 16 * (k.pair + 1))
                    for i in range(G):
                        last = act.activation(all_tile(TK, k, i), tile(ctx_c, k, i), ACT.Tanh,
                                              accum_out=per_tile(SUMK, k, i, 1))
                    last.then_inc(tanh_k, 1)
                    act.wait_ge(vT_ps, k.n + 1)
                    wait(act, P_ps, k.n - 1)
                    act.activation(buf(vT_c, k), VT_B[k.buf][:, :], ACT.Copy).then_inc(vT_sb, 1)
                k = at(1)
                if k.live:
                    act.wait_ge(P_ps, k.n + 1)
                    if is_chunk(k, 0):
                        act.wait_ge(consts, 7)
                    act.activation(pv_chunk(k), tiles(P_B[k.buf][:, :]), ACT.Copy).then_inc(P_sb, 1)
                k = at(2)
                if k.live:
                    act.wait_ge(q_ready, k.n + 1)
                    for i in range(G):
                        last = act.activation(all_tile(TQ, k, i), tile(q_c, k, i), ACT.Tanh,
                                              accum_out=per_tile(SUMQ, k, i, 1))
                    last.then_inc(tanh_q, 1)
                if is_chunk(k, 1):
                    act.wait_ge(w_ps, 1)
                    act.wait_ge(w_in, 16 * 5)
                    act.activation(W1u, bank[3][:, :], ACT.Copy)
                    act.activation(W1g, bank[3][:, :], ACT.Identity, scale=g_col[:, 0:1])
                    act.activation(W1h[:, :], bank[3][:, :], ACT.Identity, scale=g_col[:, 0:1])
                    act.activation(W2T[:, :], bank[4][:, :], ACT.Copy).then_inc(w_sb, 1)

            run_steps(act, NC, 2, phase1)

            act.preload_act_table_set("natural_log_exp_and_others")

            def phase2(at):
                k = at(0)
                if k.live:
                    wait(act, lr_ready, k.n - 1)
                    wait(act, lT_ps, k.n - 1)
                    act.activation(buf(lnq_c, k), chunk(TQ, k), ACT.Ln, bias=half_c[:, 0:1], scale=TANH_GAIN)
                    act.activation(buf(lr_c, k), chunk(TK, k), ACT.Ln, bias=half_c[:, 0:1],
                                   scale=TANH_GAIN).then_inc(ln_ready, 1)
                if is_chunk(k, 0):
                    act.wait_ge(norms, NORM_STEPS)
                    act.activation(LRATIO[:, :], NRATIO[:, :], ACT.Ln).then_inc(lratio, 1)
                k = at(1)
                if k.live:
                    wait(act, s_ps, k.n - 1)
                    act.wait_ge(dT_ps, k.n + 1)
                    act.activation(buf(dT_c, k), D_B[:, :], ACT.Copy).then_inc(dT_sb, 1)
                    act.wait_ge(lT_ps, k.n + 1)
                    act.activation(buf(lT_c, k), L_B[:, :], ACT.Copy).then_inc(lT_sb, 1)
                k = at(2)
                if k.live:
                    act.wait_ge(s_ps, k.n + 1)
                    wait(act, ep_ps, k.n - 1)
                    for h in range(2):
                        rows_h = slice(h * S, (h + 1) * S)
                        last = act.activation(tiles(buf(E_c, k))[rows_h, :, rows_h],
                                              tiles(S_B[k.buf][:, :])[rows_h, :, rows_h],
                                              ACT.Exp, scale=-float(D) ** -0.5)
                    last.then_inc(e_ready, 1)
                k = at(4)
                if k.live:
                    act.wait_ge(f_ready, k.n + 1)
                    for i in range(G):
                        last = act.activation(all_tile(TK, k, i), all_tile(F, k, i), ACT.Square,
                                              scale=float(D) ** -0.5, accum_out=per_tile(VARF, k, i, 1))
                    last.then_inc(fvar_ready, 1)

            act.wait_ge(w_done, 1)
            act.wait_ge(e_zero, 1)
            run_steps(act, NC, 4, phase2)

            act.wait_ge(fvar_ready, NC)
            act.activation(VARF[:, :], VARF[:, :], ACT.Ln, bias=eps_c[:, 0:1]).then_inc(fln_ready, 1)
            act.wait_ge(fln_ready, 1)
            act.activation(RSTDF[:, :], VARF[:, :], ACT.Exp, scale=-0.5).then_inc(frstd, 1)

            act.preload_act_table_set("gelu_and_others")
            act.wait_ge(wf_ps, 1)
            act.activation(WfT[:, :], bank[7][:, 0:D], ACT.Copy).then_inc(wf_sb, 1)

            def phase3(at):
                h, m, o, q = at(0), at(1), at(2), at(5)

                def gelu(j):
                    if m.live:
                        act.wait_ge(m1_ps, HB * m.n + (j + 1))
                        if j == 0:
                            wait(act, m2_ps, m.n - 1)
                        act.activation(buf(hid_c, m, HB * C)[:, j * C:(j + 1) * C], M1_B[j % 2][:, :], ACT.Gelu,
                                       bias=b1c[:, j:j + 1]).then_inc(gelu_ready, 1)

                gelu(0)
                gelu(1)
                if h.live:
                    act.wait_ge(hT_ps, h.n + 1)
                    wait(act, m1_ps, HB * (h.n - 1))
                    act.activation(buf(hTh, h), HT_B[:, :], ACT.Copy).then_inc(hi_ready, 1)
                if o.live:
                    act.wait_ge(o_ready, o.n + 1)
                    wait(act, oeps_ready, o.n - 1)
                    for i in range(G):
                        last = act.activation(all_tile(TK, o, i), all_tile(F, o, i), ACT.Square,
                                              scale=float(D) ** -0.5,
                                              accum_out=sso[:, o.buf * G + i:o.buf * G + i + 1])
                    last.then_inc(ovar_ready, 1)
                gelu(2)
                gelu(3)
                if q.live:
                    act.wait_ge(xqT_ps, q.n + 1)
                    wait(act, ff_ps, q.n - 1)
                    act.activation(buf(xqT_c, q), XQ_B[:, :], ACT.Copy).then_inc(xqT_sb, 1)
                    act.wait_ge(ff_ps, q.n + 1)
                    wait(act, y_ready, q.n - 1)
                    act.activation(buf(r16_c, q), FF_B[:, :], ACT.Copy).then_inc(r16_ready, 1)

            run_steps(act, NC, 5, phase3)

        @block.vector
        def _(dve):
            def centre_row(row, steps_before):
                n = steps_before
                dve.tensor_reduce(row_mean[:, :], row, AX.X, ALU.add).then_inc(row_step, 1)
                dve.wait_ge(row_step, n + 1)
                dve.tensor_scalar(row_mean[:, :], row_mean[:, :], 1.0 / D, None, ALU.mult).then_inc(row_step, 1)
                dve.wait_ge(row_step, n + 2)
                return dve.tensor_scalar(row, row, row_mean[:, :], None, ALU.subtract)

            dve.wait_ge(bd_in, 16)
            centre_row(bd_r, 0).then_inc(bd_ready, 1)

            def stats_terms(k, taken, halves):
                st = xstat[:, k.buf * G * 6:(k.buf + 1) * G * 6].rearrange("p (t s) -> p t s", s=6)
                mv = xmv[:, k.buf * G * 2:(k.buf + 1) * G * 2].rearrange("p (t s) -> p t s", s=2)
                gap = buf(xgap, k, G)
                dve.wait_ge(taken, k.n + 1)
                dve.tensor_tensor(mv, st[:, :, 1:3], st[:, :, 4:6], ALU.add)
                dve.tensor_tensor(gap, st[:, :, 1], st[:, :, 4], ALU.subtract).then_inc(halves, 1)

            def stats_halves(k, halves, terms):
                mv = xmv[:, k.buf * G * 2:(k.buf + 1) * G * 2].rearrange("p (t s) -> p t s", s=2)
                gap = buf(xgap, k, G)
                dve.wait_ge(halves, k.n + 1)
                dve.scalar_tensor_tensor(out=gap, in0=gap, scalar=0.25, in1=gap, op0=ALU.mult, op1=ALU.mult)
                dve.tensor_scalar(mv[:, :, 1], mv[:, :, 1], 1.0 / D, LN_EPS, ALU.mult, ALU.add)
                dve.tensor_scalar(mv[:, :, 0], mv[:, :, 0], 0.5, None, ALU.mult).then_inc(terms, 1)

            def stats_var(k, terms, done):
                mv = xmv[:, k.buf * G * 2:(k.buf + 1) * G * 2].rearrange("p (t s) -> p t s", s=2)
                dve.wait_ge(terms, k.n + 1)
                dve.tensor_tensor(buf(xvar, k, G), buf(xgap, k, G), mv[:, :, 1], ALU.add).then_inc(done, 1)

            def phase1(at):
                s, q, r = at(0), at(1), at(3)
                if s.live:
                    dve.wait_ge(x_in[s.buf], 16 * (s.pair + 1))
                    for i in range(G):
                        last = dve.bn_stats(xstat[:, (s.buf * G + i) * 6:(s.buf * G + i + 1) * 6], all_tile(X, s, i))
                    last.then_inc(x_bn, 1)
                if r.live:
                    dve.wait_ge(qb_ready, r.n + 1)
                    dve.wait_ge(P_sb, r.n + 1)
                    dve.tensor_tensor(tiles(chunk(F, r)), tiles(chunk(F, r)), pv_chunk(r), ALU.add).then_inc(pq_ready, 1)
                if s.live:
                    wait(dve, q_ready, s.n - 1)
                    stats_terms(s, x_bn, x_halves)
                    stats_halves(s, x_halves, x_terms)
                    stats_var(s, x_terms, x_var)
                if q.live:
                    dve.wait_ge(x_rstd, q.n + 1)
                    wait(dve, tanh_q, q.n - 1)
                    wait(dve, qb_ready, q.n - 1)
                    for i in range(G):
                        m = (q.buf * G + i) * 2
                        last = dve.tensor_scalar(tile(q_c, q, i), all_tile(X, q, i), xmv[:, m:m + 1],
                                                 xrstd[:, q.buf * G + i:q.buf * G + i + 1], ALU.subtract, ALU.mult)
                    last.then_inc(q_ready, 1)

            run_steps(dve, NC, 3, phase1)

            dve.wait_ge(w_sb, 1)
            dve.tensor_tensor(W1l[:, :], W1g, W1h[:, :].bitcast(F32), ALU.subtract)
            dve.wait_ge(b1_ps, 1)
            dve.tensor_tensor(b1c[:, :], bank[5][:, 0:HB], b1_raw[:, :], ALU.add).then_inc(w_done, 1)

            n = [0]

            def norm(ins):
                n[0] += 1
                ins.then_inc(norms, 1)
                dve.wait_ge(norms, n[0])

            dve.wait_ge(tanh_k, NC)
            dve.wait_ge(tanh_q, NC)
            norm(dve.tensor_scalar(NORM[:, :], SUM[:, :], TANH_GAIN, TANH_SHIFT * D + PROB_EPS, ALU.mult, ALU.add))
            norm(dve.reciprocal(RNORM[:, :], NORM[:, :]))
            dve.tensor_scalar(GAINS[:, T:2 * T], RNORM[:, T:2 * T], -TANH_GAIN, None, ALU.mult)
            norm(dve.tensor_tensor(SHIFT[:, :], RNORM[:, 0:T], RNORM[:, T:2 * T], ALU.subtract))
            dve.tensor_tensor(NRATIO[:, :], NORM[:, T:2 * T], RNORM[:, 0:T], ALU.mult)
            dve.tensor_scalar(GAINS[:, 0:T], RNORM[:, 0:T], TANH_GAIN, None, ALU.mult)
            norm(dve.tensor_scalar(SHIFT[:, :], SHIFT[:, :], TANH_SHIFT, None, ALU.mult))
            assert n[0] == NORM_STEPS

            def phase2(at):
                k = at(3)
                if k.live:
                    dve.wait_ge(ep_ps, k.n + 1)
                    for hb in range(2):
                        o = k.buf * G + 2 * hb
                        last = dve.reciprocal(nrden[:, o:o + 2],
                                              EP_B[k.buf][hb][:, :].rearrange("p (t w) -> p t w", w=EPW)[:, :, D])
                    last.then_inc(rden, 1)
                    dve.wait_ge(rden, k.n + 1)
                    for i in range(G):
                        ep = EP_B[k.buf][i // 2][:, (i % 2) * EPW:(i % 2) * EPW + D]
                        last = dve.scalar_tensor_tensor(out=all_tile(F, k, i), in0=ep,
                                                        scalar=nrden[:, k.buf * G + i:k.buf * G + i + 1],
                                                        in1=all_tile(F, k, i), op0=ALU.mult, op1=ALU.add)
                    last.then_inc(f_ready, 1)
                k = at(0)
                if k.live:
                    dve.wait_ge(kpart, k.n + 1)
                    for i in range(G):
                        last = dve.scalar_tensor_tensor(out=tile(diff_c, k, i), in0=all_tile(TQ, k, i),
                                                        scalar=per_tile(GAINS[:, 0:T], k, i, 1),
                                                        in1=tile(diff_c, k, i), op0=ALU.mult, op1=ALU.add)
                    last.then_inc(diff_ready, 1)
                    dve.wait_ge(ln_ready, k.n + 1)
                    for i in range(G):
                        last = dve.scalar_tensor_tensor(out=tile(lr_c, k, i), in0=tile(lnq_c, k, i),
                                                        scalar=per_tile(LRATIO, k, i, 1), in1=tile(lr_c, k, i),
                                                        op0=ALU.add, op1=ALU.subtract)
                    last.then_inc(lr_ready, 1)

            dve.wait_ge(lratio, 1)
            dve.wait_ge(pq_ready, NC)
            run_steps(dve, NC, 3, phase2)

            dve.wait_ge(rows_in, 16 * 4)
            centre_row(b2_r, 2).then_inc(rows_ready, 1)

            def phase3(at):
                h, o, x1, q = at(0), at(2), at(3), at(4)
                if h.live:
                    wait(dve, hT_ps, h.n - 1)
                    dve.tensor_tensor(tiles(buf(h_c, h)), tiles(chunk(F, h)), over_features(per_tile(RSTDF, h)),
                                      ALU.mult).then_inc(h_ready, 1)
                if o.live:
                    dve.wait_ge(m2_ps, o.n + 1)
                    dve.wait_ge(fb_ready, o.n + 1)
                    dve.tensor_tensor(chunk(F, o), M2_B[o.buf][:, :], chunk(F, o), ALU.add).then_inc(o_ready, 1)
                if x1.live:
                    dve.wait_ge(orstd_ready, x1.n + 1)
                    for i in range(G):
                        last = dve.scalar_tensor_tensor(out=all_tile(F, x1, i), in0=all_tile(F, x1, i),
                                                        scalar=orstd[:, x1.buf * G + i:x1.buf * G + i + 1],
                                                        in1=g_r, op0=ALU.mult, op1=ALU.mult)
                    last.then_inc(xn_ready, 1)
                    dve.wait_ge(xn_ready, x1.n + 1)
                    wait(dve, x1b_ready, x1.n - 1)
                    wait(dve, xq_ready, x1.n - 1)
                    dve.tensor_tensor(buf(x1_c, x1), chunk(X, x1), chunk(F, x1), ALU.add).then_inc(x1_ready, 1)
                if q.live:
                    wait(dve, xqT_ps, q.n - 1)
                    dve.wait_ge(x1_rstd, q.n + 1)
                if x1.live:
                    dve.wait_ge(x1_ready, x1.n + 1)
                    for i in range(G):
                        at_i = x1.buf * G + i
                        last = dve.bn_stats(xstat[:, at_i * 6:at_i * 6 + 6], tile(x1_c, x1, i))
                    last.then_inc(x1_bn, 1)
                if q.live:
                    for i in range(G):
                        m = (q.buf * G + i) * 2
                        last = dve.tensor_scalar(tile(xq_c, q, i), tile(x1_c, q, i), xmv[:, m:m + 1],
                                                 xrstd[:, q.buf * G + i:q.buf * G + i + 1],
                                                 ALU.subtract, ALU.mult, saturate=False)
                    last.then_inc(xq_ready, 1)
                if x1.live:
                    wait(dve, x1_rstd, x1.n - 1)
                    stats_terms(x1, x1_bn, x1_halves)
                if h.live:
                    dve.wait_ge(hi_ready, h.n + 1)
                    dve.tensor_tensor(buf(hTl, h), HT_B[:, :], buf(hTh, h).bitcast(F32),
                                      ALU.subtract).then_inc(lo_ready, 1)
                if x1.live:
                    stats_halves(x1, x1_halves, x1_terms)
                    stats_var(x1, x1_terms, x1_var)

            dve.wait_ge(xb_ready, NC)
            dve.wait_ge(frstd, 1)
            run_steps(dve, NC, 4, phase3)

        @block.tensor
        def _(pe):
            pe.wait_ge(consts, 7)
            pe.wait_ge(wd_in, 16)
            pe.matmul(bank[6][:, 0:D], Wd_raw, centre, start=True, stop=True).then_inc(wd_ps, 1)

            def phase1(at):
                k = at(1)
                if is_chunk(k, 2):
                    pe.wait_ge(w_in, 16 * 5)
                    for j in range(HB):
                        pe.transpose(bank[3][:, j * D:(j + 1) * D], W1_raw[:, j * D:(j + 1) * D], ident[:, :])
                        last = pe.matmul(bank[4][:, j * D:(j + 1) * D], W2_raw[:, j * D:(j + 1) * D], centre,
                                         start=True, stop=True)
                    last.then_inc(w_ps, 1)
                if k.live:
                    if is_chunk(k, 0):
                        pe.wait_ge(wd_sb, 1)
                    pe.wait_ge(vT_sb, k.n + 1)
                    wait(pe, P_sb, k.n - 1)
                    for i in range(G):
                        last = pe.matmul(P_B[k.buf][:, i * D:(i + 1) * D], tile(vT_c, k, i), WdT[:, :],
                                         start=True, stop=True)
                    last.then_inc(P_ps, 1)
                k = at(0)
                if k.live:
                    pe.wait_ge(ctx_sem[k.buf], 16 * (k.pair + 1))
                    wait(pe, vT_sb, k.n - 1)
                    for i in range(G):
                        last = pe.transpose(VT_B[k.buf][:, i * D:(i + 1) * D], tile(ctx_c, k, i), ident[:, :])
                    last.then_inc(vT_ps, 1)

            run_steps(pe, NC, 1, phase1)

            pe.wait_ge(w_sb, 1)
            for j in range(HB):
                last = pe.matmul(bank[5][:, j:j + 1], W1u[:, j * D:(j + 1) * D], b_col[:, :], start=True, stop=True)
            last.then_inc(b1_ps, 1)

            def phase2(at):
                k = at(1)
                if k.live:
                    pe.wait_ge(dT_sb, k.n + 1)
                    pe.wait_ge(lT_sb, k.n + 1)
                    wait(pe, e_ready, k.n - 1)
                    for i in range(G):
                        last = pe.matmul(S_B[k.buf][:, i * D:(i + 1) * D], tile(lT_c, k, i), tile(dT_c, k, i),
                                         start=True, stop=True)
                    last.then_inc(s_ps, 1)
                k = at(2)
                if k.live:
                    pe.wait_ge(e_ready, k.n + 1)
                    wait(pe, f_ready, k.n - 1)
                    for i in range(G):
                        o = (i % 2) * EPW
                        last = pe.matmul(EP_B[k.buf][i // 2][:, o:o + D + 1], tile(E_c, k, i),
                                         all_tile(PV, k, i, D + 1, D + 1), start=True, stop=True)
                    last.then_inc(ep_ps, 1)
                k = at(0)
                if k.live:
                    pe.wait_ge(diff_ready, k.n + 1)
                    wait(pe, dT_sb, k.n)
                    for i in range(G):
                        last = pe.transpose(D_B[:, i * D:(i + 1) * D], tile(diff_c, k, i), ident[:, :])
                    last.then_inc(dT_ps, 1)
                    pe.wait_ge(lr_ready, k.n + 1)
                    wait(pe, lT_sb, k.n)
                    for i in range(G):
                        last = pe.transpose(L_B[:, i * D:(i + 1) * D], tile(lr_c, k, i), ident[:, :])
                    last.then_inc(lT_ps, 1)

            pe.wait_ge(P_sb, NC)
            pe.wait_ge(w_done, 1)
            run_steps(pe, NC, 2, phase2)

            pe.wait_ge(wf_q, 1)
            pe.wait_ge(e_ready, NC)
            pe.transpose(bank[7][:, 0:D], wq[1], ident[:, :]).then_inc(wf_ps, 1)

            def phase3(at):
                h, m, q = at(0), at(1), at(5)

                def mlp1(j):
                    if m.live:
                        if j == 0:
                            pe.wait_ge(hi_ready, m.n + 1)
                            pe.wait_ge(lo_ready, m.n + 1)
                        wait(pe, gelu_ready, HB * m.n + (j - 1))
                        ps = M1_B[j % 2][:, :]
                        w_hi, w_lo = W1h[:, j * P:(j + 1) * P], W1l[:, j * P:(j + 1) * P]
                        pe.matmul(ps, w_hi, buf(hTh, m), start=True, stop=False)
                        pe.matmul(ps, w_hi, buf(hTl, m), start=False, stop=False)
                        pe.matmul(ps, w_lo, buf(hTh, m), start=False, stop=True).then_inc(m1_ps, 1)

                def mlp2(j):
                    if m.live:
                        if j == 0:
                            wait(pe, o_ready, m.n - 1)
                        pe.wait_ge(gelu_ready, HB * m.n + (j + 1))
                        for i in range(G):
                            last = pe.matmul(M2_B[m.buf][:, i * D:(i + 1) * D],
                                             buf(hid_c, m, HB * C)[:, j * C + i * D:j * C + (i + 1) * D],
                                             W2T[:, j * D:(j + 1) * D], start=(j == 0 and i == 0), stop=(j == HB - 1),
                                             skip_group_check=True)
                        if j == HB - 1:
                            last.then_inc(m2_ps, 1)

                mlp1(0)
                mlp1(1)
                if q.live:
                    pe.wait_ge(xq_ready, q.n + 1)
                    wait(pe, xqT_sb, q.n)
                if h.live:
                    pe.wait_ge(h_ready, h.n + 1)
                    wait(pe, lo_ready, h.n)
                    wait(pe, hi_ready, h.n)
                    for i in range(G):
                        last = pe.transpose(HT_B[:, i * D:(i + 1) * D], tile(h_c, h, i), ident[:, :])
                    last.then_inc(hT_ps, 1)
                if q.live:
                    for i in range(G):
                        last = pe.matmul(XQ_B[:, i * D:(i + 1) * D], tile(xq_c, q, i), ident8[:, :],
                                         start=True, stop=True)
                    last.then_inc(xqT_ps, 1)
                mlp2(0)
                mlp1(2)
                mlp2(1)
                mlp1(3)
                mlp2(2)
                mlp2(3)
                if q.live:
                    pe.wait_ge(xqT_sb, q.n + 1)
                    wait(pe, r16_ready, q.n)
                    for i in range(G):
                        last = pe.matmul(FF_B[:, i * D:(i + 1) * D], tile(xqT_c, q, i), WfT[:, :],
                                         start=True, stop=True)
                    last.then_inc(ff_ps, 1)

            pe.wait_ge(f_ready, NC)
            pe.wait_ge(consts, CONSTS)
            pe.wait_ge(wf_sb, 1)
            run_steps(pe, NC, 5, phase3)


_INS = ['x', 'ctx_1024', 'L0_xattn_W_diff', 'L0_xattn_b_diff', 'L0_xattn_ln_g', 'L0_xattn_ln_b', 'L0_xattn_W1',
        'L0_xattn_b1', 'L0_xattn_W2', 'L0_xattn_b2', 'L0_ffn_weight', 'L0_ffn_bias']


def kernel(**inputs):
    import numpy as _np
    import concourse.bacc as _bacc
    from concourse import mybir as _mybir
    from concourse.bass_utils import run_bass_kernel_spmd as _run

    nc = _bacc.Bacc("TRN2", target_bir_lowering=False, num_devices=1)
    arrays, args = {}, []
    for name in _INS:
        a = _np.ascontiguousarray(inputs[name])
        arrays[f"in_{name}_dram"] = a
        args.append(nc.dram_tensor(f"in_{name}_dram", a.shape, _mybir.dt.from_np(a.dtype), kind="ExternalInput").ap())
    shape = arrays["in_x_dram"].shape
    args.append(nc.dram_tensor("out_0_dram", shape, _mybir.dt.float32, kind="ExternalOutput").ap())
    xattn_ffn_kernel(nc, *args)
    r = _run(nc, [arrays], core_ids=[0])
    return r.results[0]["out_0_dram"]
```

```python
from contextlib import ExitStack

import concourse.bass as bass
from concourse import mybir

F32 = mybir.dt.float32
F32R = mybir.dt.float32r
BF16 = mybir.dt.bfloat16
F16 = mybir.dt.float16
F8 = mybir.dt.float8e4
ALU = mybir.AluOpType
ACT = mybir.ActivationFunctionType
AX = mybir.AxisListType

P = 128
LN_EPS = 1e-5
PROB_EPS = 1e-8
TANH_GAIN, TANH_SHIFT = 0.499, 0.5
E4M3FN_MAX = 448.0
E4M3_SAFE = 128.0


class Chunk:

    def __init__(self, half, odd, lag, chunks):
        self.n = 2 * half + (odd - lag)
        self.pair = half + (odd - lag) // 2
        self.buf = (odd - lag) % 2
        self.live = not isinstance(half, int) or 0 <= self.n < chunks


def wait(eng, sem, count):
    if isinstance(count, int) and count <= 0:
        return
    eng.wait_ge(sem, count)


def is_chunk(k, n):
    return isinstance(k.n, int) and k.n == n


def run_steps(eng, chunks, last_lag, step):
    first = (last_lag + 3) // 2
    for n in range(2 * first):
        step(lambda lag, n=n: Chunk(n // 2, n % 2, lag, chunks))
    with eng.Fori(first, chunks // 2) as half:
        for odd in range(2):
            step(lambda lag, odd=odd: Chunk(half, odd, lag, chunks))
    for n in range(chunks, chunks + last_lag):
        step(lambda lag, n=n: Chunk(n // 2, n % 2, lag, chunks))


def xattn_ffn_kernel(nc, x, ctx_in, W_diff, b_diff, ln_g, ln_b, W1, b1, W2, b2, Wf, bf, out):
    B, S, D = x.shape
    HID = W1.shape[0]
    HB = HID // P
    assert D == P and 2 * S == P
    T = B * S // P
    G = 4
    C = G * D
    NC = T // G
    EPW = 256

    x_d = x.rearrange("b s d -> (b s) d").rearrange("(c t p) d -> c p t d", t=G, p=P)
    ctx_d = ctx_in.rearrange("b s d -> (b s) d").rearrange("(c t p) d -> c p t d", t=G, p=P)
    out_d = out.rearrange("b s d -> (b s) d").rearrange("(c t p) d -> c p t d", t=G, p=P)

    with ExitStack() as ctx:
        def sb(name, shape, dt=F32):
            return ctx.enter_context(nc.sbuf_tensor(name, shape, dt))

        def sem(name):
            return ctx.enter_context(nc.semaphore(name))

        bank = [ctx.enter_context(nc.psum_tensor(f"bank{i}", [P, 512], F32)) for i in range(8)]

        X = sb("X", [P, T * D])
        TQK = sb("TQK", [P, 2 * T * D])
        TQ = TQK[:, 0:T * D]
        TK = TQK[:, T * D:2 * T * D]
        F = sb("F", [P, T * D])
        PV = sb("PV", [P, T * (D + 1)])
        SUM = sb("SUM", [P, 2 * T])
        SUMQ, SUMK = SUM[:, 0:T], SUM[:, T:2 * T]
        NORM = sb("NORM", [P, 2 * T])
        RNORM = sb("RNORM", [P, 2 * T])
        GAINQ = sb("GAINQ", [P, T])
        GAINK = sb("GAINK", [P, T])
        HALFK = sb("HALFK", [P, T])
        SHIFT = sb("SHIFT", [P, T])
        NRATIO = sb("NRATIO", [P, T])
        LRATIO = sb("LRATIO", [P, T])
        VARF = sb("VARF", [P, T])
        RSTDF = sb("RSTDF", [P, T])

        ident = sb("ident", [P, P])
        half_c = sb("half_c", [P, 1])
        pow_c = sb("pow_c", [P, 2 * G])
        eps_c = sb("eps_c", [P, 2 * G])
        WdT = sb("WdT", [P, D])
        W1h = sb("W1h", [P, HID], F32R)
        W1l = sb("W1l", [P, HID], F32R)
        b1c = sb("b1c", [P, HB])
        b1_raw = sb("b1_raw", [P, HB])
        W2T = sb("W2T", [P, HB * D])
        Wf_raw = sb("Wf_raw", [P, D])
        Wf8 = sb("Wf8", [P, D], F8)
        WfT = sb("WfT", [P, D], BF16)
        ident8 = sb("ident8", [P, P], F8)
        rows = sb("rows", [P, 5 * D])
        bd_r, b2_r, g_r, b_r, bf_r = (rows[:, i * D:(i + 1) * D] for i in range(5))
        row_mean = sb("row_mean", [P, 1])
        g_col = sb("g_col", [P, 1])
        b_col = sb("b_col", [P, 1])

        LN_c = sb("LN_c", [P, 4 * C])
        ctx_c = LN_c[:, 0:2 * C]
        q_c = sb("q_c", [P, 2 * C])
        vT_c = sb("vT_c", [P, 2 * C])
        diff_c, dT_c = q_c, vT_c
        lT_c = sb("lT_c", [P, 2 * C])
        E_c = sb("E_c", [P, 2 * C])
        hTh = sb("hTh", [P, 2 * C], F32R)
        hTl = sb("hTl", [P, 2 * C], F32R)
        xstat = sb("xstat", [P, 2 * G * 6])
        xmv = sb("xmv", [P, 2 * G * 2])
        xgap = sb("xgap", [P, 2 * G])
        xvar = sb("xvar", [P, 2 * G])
        xrstd = sb("xrstd", [P, 2 * G])
        nrden = sb("nrden", [P, 2 * G])
        sso = sb("sso", [P, 2 * G])
        ovar = sb("ovar", [P, 2 * G])
        orstd = sb("orstd", [P, 2 * G])

        hid_c = TQ[:, 0:2 * HB * C]
        h_c = q_c
        x1_c = vT_c
        xq_c = ctx_c[:, 0:C // 2].bitcast(F8)
        xqT_c = ctx_c[:, C:2 * C].bitcast(BF16)
        r16_c = LN_c[:, 2 * C:3 * C].bitcast(F16)

        Wd_raw = E_c[:, 0:D]
        W1_raw, W1u = LN_c[:, 2 * C:2 * C + HB * D], LN_c[:, 3 * C:3 * C + HID]
        W2_raw = lT_c[:, 0:HID]
        wq = [SUM[:, :], NORM[:, :], RNORM[:, :]]
        centre = E_c[:, D:2 * D]
        VT_B, P_B = (bank[0], bank[7]), (bank[1], bank[2])
        D_B, L_B, S_B, EP_B = bank[2], bank[3], (bank[4], bank[7]), ((bank[5], bank[6]), (bank[0], bank[1]))
        M1_B, M2_B, HT_B, XQ_B, FF_B = (bank[0], bank[1]), (bank[2], bank[3]), bank[4], bank[5], bank[6]

        def chunk(t, k, width=C):
            return t[:, bass.ds(k.n * width, width)] if not isinstance(k.n, int) else t[:, k.n * width:(k.n + 1) * width]

        def buf(t, k, width=C):
            return t[:, k.buf * width:(k.buf + 1) * width]

        def tile(t, k, i):
            return t[:, k.buf * C + i * D:k.buf * C + (i + 1) * D]

        def tanh_both(k):
            sides = TQK[:, :].rearrange("p (s c) -> p s c", s=2)
            at = k.n * C
            return sides[:, :, bass.ds(at, C)] if not isinstance(at, int) else sides[:, :, at:at + C]

        def ln_tile(side, k, i):
            at = (2 * k.buf + side) * C + i * D
            return LN_c[:, at:at + D]

        def tiles(ap):
            return ap.rearrange("p (t d) -> p t d", d=D)

        def per_tile(t, k, i=0, n=G):
            at = k.n * G + i
            return t[:, bass.ds(at, n)] if not isinstance(at, int) else t[:, at:at + n]

        def all_tile(t, k, i, width=D, stride=D):
            at = (k.n * G + i) * stride
            return t[:, bass.ds(at, width)] if not isinstance(at, int) else t[:, at:at + width]

        def over_tiles(row):
            return row.unsqueeze(1).broadcast_to([P, G, D])

        def over_features(col):
            return col.unsqueeze(2).broadcast_to([P, G, D])

        def pv_chunk(k):
            w = D + 1
            at = k.n * G * w
            ap = PV[:, bass.ds(at, G * w)] if not isinstance(at, int) else PV[:, at:at + G * w]
            return ap.rearrange("p (t w) -> p t w", w=w)[:, :, 0:D]

        wd_in, bd_in, rows_in, w_in, wf_in, consts = (
            sem("wd_in"), sem("bd_in"), sem("rows_in"), sem("w_in"), sem("wf_in"), sem("consts"))
        row_step, bd_ready, b1_ready = sem("row_step"), sem("bd_ready"), sem("b1_ready")
        rows_ready, wd_ps, wd_sb, w_ps, w_sb = (
            sem("rows_ready"), sem("wd_ps"), sem("wd_sb"), sem("w_ps"), sem("w_sb"))
        b1_ps, w_done, wf_step, wf_q, wf_ps, wf_sb, fb_ready, e_zero = (
            sem("b1_ps"), sem("w_done"), sem("wf_step"), sem("wf_q"), sem("wf_ps"), sem("wf_sb"),
            sem("fb_ready"), sem("e_zero"))
        x_in = [sem(f"x_in{i}") for i in range(2)]
        ctx_sem = [sem(f"ctx_in{i}") for i in range(2)]
        x_bn, x_halves, x_terms = sem("x_bn"), sem("x_halves"), sem("x_terms")
        x_var, x_rstd, xb_ready = sem("x_var"), sem("x_rstd"), sem("xb_ready")
        q_ready, qb_ready, pq_ready = sem("q_ready"), sem("qb_ready"), sem("pq_ready")
        tanh_k, tanh_q = sem("tanh_k"), sem("tanh_q")
        vT_ps, vT_sb, P_ps, P_sb = sem("vT_ps"), sem("vT_sb"), sem("P_ps"), sem("P_sb")
        norm_step, halfk_ready, norms, lratio = sem("norm_step"), sem("halfk_ready"), sem("norms"), sem("lratio")
        kscaled = sem("kscaled")
        kpart, ln_ready, diff_ready, lr_ready = sem("kpart"), sem("ln_ready"), sem("diff_ready"), sem("lr_ready")
        dT_ps, dT_sb, lT_ps, lT_sb = sem("dT_ps"), sem("dT_sb"), sem("lT_ps"), sem("lT_sb")
        s_ps, e_ready, ep_ps, rden, f_ready = sem("s_ps"), sem("e_ready"), sem("ep_ps"), sem("rden"), sem("f_ready")
        fvar_ready, feps_ready = sem("fvar_ready"), sem("feps_ready")
        h_ready, hT_ps, hi_ready, lo_ready = sem("h_ready"), sem("hT_ps"), sem("hi_ready"), sem("lo_ready")
        m1_ps, gelu_ready, m2_ps, o_ready = sem("m1_ps"), sem("gelu_ready"), sem("m2_ps"), sem("o_ready")
        fln_ready, frstd, ovar_ready, oeps_ready, orstd_ready = (
            sem("fln_ready"), sem("frstd"), sem("ovar_ready"), sem("oeps_ready"), sem("orstd_ready"))
        xn_ready, x1_ready, x1_bn, x1_halves, x1_terms, x1_var, x1_rstd = (
            sem("xn_ready"), sem("x1_ready"), sem("x1_bn"), sem("x1_halves"), sem("x1_terms"), sem("x1_var"),
            sem("x1_rstd"))
        x1b_ready, xq_ready, xqT_ps, xqT_sb, ff_ps, r16_ready, y_ready = (
            sem("x1b_ready"), sem("xq_ready"), sem("xqT_ps"), sem("xqT_sb"), sem("ff_ps"), sem("r16_ready"),
            sem("y_ready"))
        stored = sem("stored")

        CONSTS = 8
        EARLY = NC - 2
        block = ctx.enter_context(nc.Block())

        @block.sync
        def _(sp):
            def load(k):
                wait(sp, tanh_k, k.n - 1)
                wait(sp, vT_ps, k.n - 1)
                sp.dma_start(tiles(buf(ctx_c, k)), ctx_d[k.n]).then_inc(ctx_sem[k.buf], 16)
                wait(sp, x_var, k.n - 1)
                sp.dma_start(tiles(chunk(X, k)), x_d[k.n]).then_inc(x_in[k.buf], 16)

            for n in range(2):
                load(Chunk(0, n, 0, NC))
            sp.dma_start(W1_raw.rearrange("p (j d) -> p j d", d=D),
                         W1.rearrange("(j p) d -> p j d", p=P)).then_inc(w_in, 16)
            sp.dma_start(W2_raw, W2).then_inc(w_in, 16)
            sp.dma_start(g_col[:, :], ln_g.unsqueeze(1), allow_slow_non_contiguous=True).then_inc(w_in, 16)
            sp.dma_start(b_col[:, :], ln_b.unsqueeze(1), allow_slow_non_contiguous=True).then_inc(w_in, 16)
            sp.dma_start(b1_raw[:, :], b1.rearrange("(j p) -> p j", p=P),
                         allow_slow_non_contiguous=True).then_inc(w_in, 16)
            for n in range(2, 4):
                load(Chunk(n // 2, n % 2, 0, NC))
            for row, vec in ((b2_r, b2), (g_r, ln_g), (b_r, ln_b), (bf_r, bf)):
                sp.dma_start(row, vec.unsqueeze(0).broadcast_to([P, D])).then_inc(rows_in, 16)
            sp.dma_start(Wf_raw[:, :], Wf).then_inc(wf_in, 16)
            with sp.Fori(2, NC // 2) as half:
                for odd in range(2):
                    load(Chunk(half, odd, 0, NC))

            def store(k):
                wait(sp, y_ready, k.n + 1)
                sp.dma_start(out_d[k.n], tiles(chunk(F, k))).then_inc(stored, 16)

            with sp.Fori(0, NC // 2) as half:
                for odd in range(2):
                    store(Chunk(half, odd, 0, NC))
            sp.wait_ge(stored, 16 * NC)

        @block.gpsimd
        def _(pool):
            pool.memset(ident[:, :], 0.0).then_inc(consts, 1)
            pool.wait_ge(consts, 1)
            pool.affine_select(out=ident[:, :], in_=ident[:, :], compare_op=ALU.not_equal, fill=1.0,
                               base=0, pattern=[[-1, P]], channel_multiplier=1).then_inc(consts, 1)
            pool.memset(pow_c[:, :], -0.5).then_inc(consts, 1)
            pool.wait_ge(consts, 3)
            pool.tensor_scalar(centre, ident[:, :], -1.0 / D, None, ALU.add).then_inc(consts, 1)
            pool.memset(eps_c[:, :], LN_EPS).then_inc(consts, 1)
            pool.tensor_copy(ident8[:, :], ident[:, :], saturate=False).then_inc(consts, 1)
            pool.memset(half_c[:, :], TANH_SHIFT).then_inc(consts, 1)
            pool.memset(PV[:, :].rearrange("p (t w) -> p t w", w=D + 1)[:, :, D:D + 1], -1.0).then_inc(consts, 1)

            def phase1(at):
                k = at(0)
                if k.live:
                    pool.wait_ge(x_var, k.n + 1)
                    wait(pool, q_ready, k.n - 1)
                    pool.tensor_tensor(buf(xrstd, k, G), buf(xvar, k, G), pow_c[:, 0:G], ALU.pow).then_inc(x_rstd, 1)
                k = at(1)
                if k.live:
                    pool.wait_ge(q_ready, k.n + 1)
                    pool.tensor_tensor(tiles(chunk(F, k)), tiles(buf(q_c, k)), over_tiles(bd_r),
                                       ALU.add).then_inc(qb_ready, 1)
                if is_chunk(k, 2):
                    pool.wait_ge(w_ps, 1)
                    pool.memset(E_c[:, :], 0.0).then_inc(e_zero, 1)

            pool.wait_ge(bd_ready, 1)
            run_steps(pool, NC, 1, phase1)

            def phase2(at):
                k = at(0)
                if k.live:
                    wait(pool, dT_ps, k.n - 1)
                    if is_chunk(k, 1):
                        pool.wait_ge(tanh_q, NC)
                        pool.wait_ge(norms, 2)
                    pool.tensor_tensor(tiles(buf(diff_c, k)), tiles(chunk(TK, k)),
                                       over_features(per_tile(GAINK, k)), ALU.mult).then_inc(kscaled, 1)
                    pool.wait_ge(kscaled, k.n + 1)
                    pool.tensor_tensor(tiles(buf(diff_c, k)), tiles(buf(diff_c, k)),
                                       over_features(per_tile(SHIFT, k)), ALU.add).then_inc(kpart, 1)
                k = at(2)
                if k.live:
                    pool.tensor_tensor(tiles(chunk(X, k)), tiles(chunk(X, k)), over_tiles(b_r),
                                       ALU.add).then_inc(xb_ready, 1)

            pool.wait_ge(norms, 1)
            pool.wait_ge(qb_ready, NC)
            pool.wait_ge(tanh_q, NC - 1)
            run_steps(pool, NC, 2, phase2)

            n = [0]

            def link(ins):
                n[0] += 1
                ins.then_inc(wf_step, 1)
                pool.wait_ge(wf_step, n[0])

            pool.wait_ge(wf_in, 16)
            link(pool.tensor_scalar(wq[0], Wf_raw[:, :], E4M3FN_MAX, -E4M3FN_MAX, ALU.min, ALU.max))
            link(pool.tensor_scalar(wq[1], wq[0], E4M3_SAFE, -E4M3_SAFE, ALU.min, ALU.max))
            link(pool.tensor_copy(Wf8[:, :], wq[1], saturate=False))
            link(pool.tensor_copy(wq[1], Wf8[:, :]))
            link(pool.tensor_scalar(wq[2], wq[0], 0.5, None, ALU.mult))
            link(pool.tensor_copy(Wf8[:, :], wq[2], saturate=False))
            link(pool.tensor_copy(wq[2], Wf8[:, :]))
            link(pool.tensor_scalar(wq[2], wq[2], 2.0, None, ALU.mult))
            link(pool.tensor_tensor(wq[0], wq[0], wq[0], ALU.mult))
            link(pool.tensor_scalar(wq[0], wq[0], E4M3_SAFE * E4M3_SAFE, None, ALU.is_gt))
            link(pool.tensor_tensor(wq[2], wq[2], wq[1], ALU.subtract))
            link(pool.tensor_tensor(wq[2], wq[2], wq[0], ALU.mult))
            pool.tensor_tensor(wq[1], wq[1], wq[2], ALU.add).then_inc(wf_q, 1)

            def phase3(at):
                k = at(4)
                if k.live:
                    pool.wait_ge(x1_ready, k.n + 1)
                    pool.tensor_tensor(tiles(chunk(F, k)), tiles(buf(x1_c, k)), over_tiles(bf_r),
                                       ALU.add).then_inc(x1b_ready, 1)
                k = at(2)
                if k.live:
                    pool.wait_ge(ovar_ready, k.n + 1)
                    wait(pool, xn_ready, k.n - 1)
                    pool.tensor_tensor(buf(ovar, k, G), buf(sso, k, G), eps_c[:, 0:G], ALU.add).then_inc(oeps_ready, 1)
                    pool.wait_ge(oeps_ready, k.n + 1)
                    pool.tensor_tensor(buf(orstd, k, G), buf(ovar, k, G), pow_c[:, 0:G], ALU.pow).then_inc(orstd_ready, 1)
                k = at(6)
                if k.live:
                    pool.wait_ge(r16_ready, k.n + 1)
                    pool.wait_ge(x1b_ready, k.n + 1)
                    pool.tensor_tensor(chunk(F, k), buf(r16_c, k), chunk(F, k), ALU.add).then_inc(y_ready, 1)
                k = at(0)
                if k.live:
                    pool.wait_ge(h_ready, k.n + 1)
                    pool.tensor_tensor(tiles(chunk(F, k)), tiles(chunk(F, k)), over_tiles(b2_r),
                                       ALU.add).then_inc(fb_ready, 1)
                k = at(3)
                if k.live:
                    pool.wait_ge(x1_var, k.n + 1)
                    wait(pool, xq_ready, k.n - 1)
                    pool.tensor_tensor(buf(xrstd, k, G), buf(xvar, k, G), pow_c[:, 0:G], ALU.pow).then_inc(x1_rstd, 1)

            late = slice(EARLY * G, NC * G)
            pool.wait_ge(fvar_ready, NC)
            pool.tensor_tensor(VARF[:, late], VARF[:, late], eps_c[:, :], ALU.add).then_inc(feps_ready, 1)
            pool.wait_ge(feps_ready, 1)
            pool.tensor_tensor(RSTDF[:, late], VARF[:, late], pow_c[:, :], ALU.pow).then_inc(frstd, 1)

            pool.wait_ge(rows_ready, 1)
            run_steps(pool, NC, 6, phase3)

        @block.scalar
        def _(act):
            act.dma_start(Wd_raw, W_diff).then_inc(wd_in, 16)
            act.dma_start(bd_r, b_diff.unsqueeze(0).broadcast_to([P, D])).then_inc(bd_in, 16)
            act.wait_ge(wd_ps, 1)
            act.activation(WdT[:, :], bank[6][:, 0:D], ACT.Copy).then_inc(wd_sb, 1)

            def phase1(at):
                k = at(0)
                if k.live:
                    act.wait_ge(ctx_sem[k.buf], 16 * (k.pair + 1))
                    for i in range(G):
                        last = act.activation(all_tile(TK, k, i), tile(ctx_c, k, i), ACT.Tanh,
                                              accum_out=per_tile(SUMK, k, i, 1))
                    last.then_inc(tanh_k, 1)
                    act.wait_ge(vT_ps, k.n + 1)
                    wait(act, P_ps, k.n - 1)
                    act.activation(buf(vT_c, k), VT_B[k.buf][:, :], ACT.Copy).then_inc(vT_sb, 1)
                k = at(1)
                if k.live:
                    act.wait_ge(P_ps, k.n + 1)
                    if is_chunk(k, 0):
                        act.wait_ge(consts, CONSTS)
                    act.activation(pv_chunk(k), tiles(P_B[k.buf][:, :]), ACT.Copy).then_inc(P_sb, 1)
                k = at(2)
                if k.live:
                    act.wait_ge(q_ready, k.n + 1)
                    for i in range(G):
                        last = act.activation(all_tile(TQ, k, i), tile(q_c, k, i), ACT.Tanh,
                                              accum_out=per_tile(SUMQ, k, i, 1))
                    last.then_inc(tanh_q, 1)
                if is_chunk(k, 0):
                    act.wait_ge(w_ps, 1)
                    act.wait_ge(w_in, 16 * 5)
                    act.activation(W1u, bank[3][:, :], ACT.Copy)
                    act.activation(W1h[:, :], bank[3][:, :], ACT.Identity, scale=g_col[:, 0:1])
                    act.activation(W2T[:, :], bank[4][:, :], ACT.Copy).then_inc(w_sb, 1)

            run_steps(act, NC, 2, phase1)

            act.preload_act_table_set("natural_log_exp_and_others")

            def upper_half(h):
                act.wait_ge(hT_ps, h.n + 1)
                wait(act, m1_ps, HB * (h.n - 1))
                act.activation(buf(hTh, h), HT_B[:, :], ACT.Copy).then_inc(hi_ready, 1)

            def phase2(at):
                k = at(0)
                if k.live:
                    wait(act, lr_ready, k.n - 1)
                    wait(act, lT_ps, k.n - 1)
                    act.activation(LN_c[:, k.buf * 2 * C:(k.buf + 1) * 2 * C].rearrange("p (s c) -> p s c", s=2),
                                   tanh_both(k), ACT.Ln, bias=half_c[:, 0:1], scale=TANH_GAIN).then_inc(ln_ready, 1)
                if is_chunk(k, 0):
                    act.wait_ge(norms, 2)
                    act.activation(LRATIO[:, :], NRATIO[:, :], ACT.Ln).then_inc(lratio, 1)
                k = at(2)
                if k.live:
                    act.wait_ge(s_ps, k.n + 1)
                    wait(act, ep_ps, k.n - 1)
                    for h in range(2):
                        rows_h = slice(h * S, (h + 1) * S)
                        last = act.activation(tiles(buf(E_c, k))[rows_h, :, rows_h],
                                              tiles(S_B[k.buf][:, :])[rows_h, :, rows_h],
                                              ACT.Exp, scale=-float(D) ** -0.5)
                    last.then_inc(e_ready, 1)
                if is_chunk(k, NC - 1):
                    act.preload_act_table_set("gelu_and_others")
                k = at(1)
                if k.live:
                    wait(act, s_ps, k.n - 1)
                    act.wait_ge(dT_ps, k.n + 1)
                    act.activation(buf(dT_c, k), D_B[:, :], ACT.Copy).then_inc(dT_sb, 1)
                    act.wait_ge(lT_ps, k.n + 1)
                    act.activation(buf(lT_c, k), L_B[:, :], ACT.Copy).then_inc(lT_sb, 1)
                k = at(3)
                if is_chunk(k, NC - 2):
                    upper_half(Chunk(0, 0, 0, NC))
                if k.live:
                    act.wait_ge(f_ready, k.n + 1)
                    for i in range(G):
                        last = act.activation(all_tile(TK, k, i), all_tile(F, k, i), ACT.Square,
                                              scale=float(D) ** -0.5, accum_out=per_tile(VARF, k, i, 1))
                    last.then_inc(fvar_ready, 1)
                if is_chunk(k, EARLY - 1):
                    cols = slice(0, EARLY * G)
                    act.wait_ge(fvar_ready, EARLY)
                    act.activation(VARF[:, cols], VARF[:, cols], ACT.Ln, bias=eps_c[:, 0:1]).then_inc(fln_ready, 1)
                    act.wait_ge(fln_ready, 1)
                    act.activation(RSTDF[:, cols], VARF[:, cols], ACT.Exp, scale=-0.5).then_inc(frstd, 1)

            act.wait_ge(w_done, 1)
            act.wait_ge(b1_ready, 1)
            act.wait_ge(e_zero, 1)
            run_steps(act, NC, 3, phase2)


            def phase3(at):
                h, m, o, q = at(0), at(1), at(2), at(5)

                def gelu(j):
                    if m.live:
                        act.wait_ge(m1_ps, HB * m.n + (j + 1))
                        if j == 0:
                            wait(act, m2_ps, m.n - 1)
                        act.activation(buf(hid_c, m, HB * C)[:, j * C:(j + 1) * C], M1_B[j % 2][:, :], ACT.Gelu,
                                       bias=b1c[:, j:j + 1]).then_inc(gelu_ready, 1)

                gelu(0)
                gelu(1)
                if is_chunk(m, 0):
                    act.wait_ge(wf_ps, 1)
                    act.activation(WfT[:, :], bank[7][:, 0:D], ACT.Copy).then_inc(wf_sb, 1)
                if h.live and not is_chunk(h, 0):
                    upper_half(h)
                if o.live:
                    act.wait_ge(o_ready, o.n + 1)
                    wait(act, oeps_ready, o.n - 1)
                    for i in range(G):
                        last = act.activation(all_tile(TK, o, i), all_tile(F, o, i), ACT.Square,
                                              scale=float(D) ** -0.5,
                                              accum_out=sso[:, o.buf * G + i:o.buf * G + i + 1])
                    last.then_inc(ovar_ready, 1)
                gelu(2)
                gelu(3)
                if q.live:
                    act.wait_ge(xqT_ps, q.n + 1)
                    wait(act, ff_ps, q.n - 1)
                    act.activation(buf(xqT_c, q), XQ_B[:, :], ACT.Copy).then_inc(xqT_sb, 1)
                    act.wait_ge(ff_ps, q.n + 1)
                    wait(act, y_ready, q.n - 1)
                    act.activation(buf(r16_c, q), FF_B[:, :], ACT.Copy).then_inc(r16_ready, 1)

            run_steps(act, NC, 5, phase3)

        @block.vector
        def _(dve):
            def centre_row(row, steps_before):
                n = steps_before
                dve.tensor_reduce(row_mean[:, :], row, AX.X, ALU.add).then_inc(row_step, 1)
                dve.wait_ge(row_step, n + 1)
                dve.tensor_scalar(row_mean[:, :], row_mean[:, :], 1.0 / D, None, ALU.mult).then_inc(row_step, 1)
                dve.wait_ge(row_step, n + 2)
                return dve.tensor_scalar(row, row, row_mean[:, :], None, ALU.subtract)

            dve.wait_ge(bd_in, 16)
            centre_row(bd_r, 0).then_inc(bd_ready, 1)

            def stats_terms(k, taken, halves):
                st = xstat[:, k.buf * G * 6:(k.buf + 1) * G * 6].rearrange("p (t s) -> p t s", s=6)
                mv = xmv[:, k.buf * G * 2:(k.buf + 1) * G * 2].rearrange("p (t s) -> p t s", s=2)
                gap = buf(xgap, k, G)
                dve.wait_ge(taken, k.n + 1)
                dve.tensor_tensor(mv, st[:, :, 1:3], st[:, :, 4:6], ALU.add)
                dve.tensor_tensor(gap, st[:, :, 1], st[:, :, 4], ALU.subtract).then_inc(halves, 1)

            def stats_halves(k, halves, terms):
                mv = xmv[:, k.buf * G * 2:(k.buf + 1) * G * 2].rearrange("p (t s) -> p t s", s=2)
                gap = buf(xgap, k, G)
                dve.wait_ge(halves, k.n + 1)
                dve.scalar_tensor_tensor(out=gap, in0=gap, scalar=0.25, in1=gap, op0=ALU.mult, op1=ALU.mult)
                dve.tensor_scalar(mv[:, :, 1], mv[:, :, 1], 1.0 / D, LN_EPS, ALU.mult, ALU.add)
                dve.tensor_scalar(mv[:, :, 0], mv[:, :, 0], 0.5, None, ALU.mult).then_inc(terms, 1)

            def stats_var(k, terms, done):
                mv = xmv[:, k.buf * G * 2:(k.buf + 1) * G * 2].rearrange("p (t s) -> p t s", s=2)
                dve.wait_ge(terms, k.n + 1)
                dve.tensor_tensor(buf(xvar, k, G), buf(xgap, k, G), mv[:, :, 1], ALU.add).then_inc(done, 1)

            def take_norms(first, end, part):
                cols, n = slice(first * G, end * G), 2 * part
                sums, norm, rnorm = (t[:, :].rearrange("p (s t) -> p s t", s=2)[:, :, cols] for t in (SUM, NORM, RNORM))
                dve.wait_ge(tanh_k, end)
                dve.wait_ge(tanh_q, end)
                dve.tensor_scalar(norm, sums, TANH_GAIN, TANH_SHIFT * D + PROB_EPS,
                                  ALU.mult, ALU.add).then_inc(norm_step, 1)
                dve.wait_ge(norm_step, n + 1)
                dve.reciprocal(rnorm, norm).then_inc(norm_step, 1)
                dve.wait_ge(norm_step, n + 2)
                dve.tensor_scalar(HALFK[:, cols], rnorm[:, 1], TANH_SHIFT, None, ALU.mult).then_inc(halfk_ready, 1)
                dve.tensor_scalar(GAINK[:, cols], rnorm[:, 1], -TANH_GAIN, None, ALU.mult)
                dve.tensor_scalar(GAINQ[:, cols], rnorm[:, 0], TANH_GAIN, None, ALU.mult)
                dve.tensor_tensor(NRATIO[:, cols], norm[:, 1], rnorm[:, 0], ALU.mult)
                dve.wait_ge(halfk_ready, part + 1)
                dve.scalar_tensor_tensor(out=SHIFT[:, cols], in0=rnorm[:, 0], scalar=TANH_SHIFT, in1=HALFK[:, cols],
                                         op0=ALU.mult, op1=ALU.subtract).then_inc(norms, 1)
                dve.wait_ge(norms, part + 1)

            def phase1(at):
                s, q, r = at(0), at(1), at(3)
                if s.live:
                    dve.wait_ge(x_in[s.buf], 16 * (s.pair + 1))
                    for i in range(G):
                        last = dve.bn_stats(xstat[:, (s.buf * G + i) * 6:(s.buf * G + i + 1) * 6], all_tile(X, s, i))
                    last.then_inc(x_bn, 1)
                if r.live:
                    dve.wait_ge(qb_ready, r.n + 1)
                    dve.wait_ge(P_sb, r.n + 1)
                    dve.tensor_tensor(tiles(chunk(F, r)), tiles(chunk(F, r)), pv_chunk(r), ALU.add).then_inc(pq_ready, 1)
                if is_chunk(q, NC - 1):
                    dve.wait_ge(w_sb, 1)
                    dve.scalar_tensor_tensor(out=W1l[:, :], in0=bank[3][:, :], scalar=g_col[:, 0:1],
                                             in1=W1h[:, :].bitcast(F32), op0=ALU.mult,
                                             op1=ALU.subtract).then_inc(w_done, 1)
                if s.live:
                    wait(dve, q_ready, s.n - 1)
                    stats_terms(s, x_bn, x_halves)
                    stats_halves(s, x_halves, x_terms)
                    stats_var(s, x_terms, x_var)
                if q.live:
                    dve.wait_ge(x_rstd, q.n + 1)
                    wait(dve, tanh_q, q.n - 1)
                    wait(dve, qb_ready, q.n - 1)
                    for i in range(G):
                        m = (q.buf * G + i) * 2
                        last = dve.tensor_scalar(tile(q_c, q, i), all_tile(X, q, i), xmv[:, m:m + 1],
                                                 xrstd[:, q.buf * G + i:q.buf * G + i + 1], ALU.subtract, ALU.mult)
                    last.then_inc(q_ready, 1)
                if is_chunk(r, EARLY - 1):
                    take_norms(0, EARLY, 0)
                    dve.wait_ge(b1_ps, 1)
                    dve.tensor_tensor(b1c[:, :], bank[5][:, 0:HB], b1_raw[:, :], ALU.add).then_inc(b1_ready, 1)

            run_steps(dve, NC, 3, phase1)

            take_norms(EARLY, NC, 1)
            def take_h(h):
                wait(dve, hT_ps, h.n - 1)
                dve.tensor_tensor(tiles(buf(h_c, h)), tiles(chunk(F, h)), over_features(per_tile(RSTDF, h)),
                                  ALU.mult).then_inc(h_ready, 1)

            def phase2(at):
                k = at(0)
                if k.live:
                    dve.wait_ge(kpart, k.n + 1)
                    for i in range(G):
                        last = dve.scalar_tensor_tensor(out=tile(diff_c, k, i), in0=all_tile(TQ, k, i),
                                                        scalar=per_tile(GAINQ, k, i, 1),
                                                        in1=tile(diff_c, k, i), op0=ALU.mult, op1=ALU.add)
                    last.then_inc(diff_ready, 1)
                    dve.wait_ge(ln_ready, k.n + 1)
                    if is_chunk(k, 0):
                        dve.wait_ge(lratio, 1)
                    for i in range(G):
                        last = dve.scalar_tensor_tensor(out=ln_tile(1, k, i), in0=ln_tile(0, k, i),
                                                        scalar=per_tile(LRATIO, k, i, 1), in1=ln_tile(1, k, i),
                                                        op0=ALU.add, op1=ALU.subtract)
                    last.then_inc(lr_ready, 1)
                k = at(2)
                if k.live:
                    dve.wait_ge(ep_ps, k.n + 1)
                    for hb in range(2):
                        o = k.buf * G + 2 * hb
                        last = dve.reciprocal(nrden[:, o:o + 2],
                                              EP_B[k.buf][hb][:, :].rearrange("p (t w) -> p t w", w=EPW)[:, :, D])
                    last.then_inc(rden, 1)
                    dve.wait_ge(rden, k.n + 1)
                    for i in range(G):
                        ep = EP_B[k.buf][i // 2][:, (i % 2) * EPW:(i % 2) * EPW + D]
                        last = dve.scalar_tensor_tensor(out=all_tile(F, k, i), in0=ep,
                                                        scalar=nrden[:, k.buf * G + i:k.buf * G + i + 1],
                                                        in1=all_tile(F, k, i), op0=ALU.mult, op1=ALU.add)
                    last.then_inc(f_ready, 1)
                if is_chunk(k, NC - 2):
                    dve.wait_ge(frstd, 1)
                    take_h(Chunk(0, 0, 0, NC))
                    dve.wait_ge(rows_in, 16 * 4)
                    centre_row(b2_r, 2).then_inc(rows_ready, 1)

            dve.wait_ge(pq_ready, NC)
            run_steps(dve, NC, 2, phase2)

            def output(o):
                if o.live:
                    dve.wait_ge(m2_ps, o.n + 1)
                    dve.wait_ge(fb_ready, o.n + 1)
                    dve.tensor_tensor(chunk(F, o), M2_B[o.buf][:, :], chunk(F, o), ALU.add).then_inc(o_ready, 1)

            def residual(x1):
                if x1.live:
                    dve.wait_ge(orstd_ready, x1.n + 1)
                    for i in range(G):
                        last = dve.scalar_tensor_tensor(out=all_tile(F, x1, i), in0=all_tile(F, x1, i),
                                                        scalar=orstd[:, x1.buf * G + i:x1.buf * G + i + 1],
                                                        in1=g_r, op0=ALU.mult, op1=ALU.mult)
                    last.then_inc(xn_ready, 1)
                    dve.wait_ge(xn_ready, x1.n + 1)
                    wait(dve, x1b_ready, x1.n - 1)
                    wait(dve, xq_ready, x1.n - 1)
                    dve.tensor_tensor(buf(x1_c, x1), chunk(X, x1), chunk(F, x1), ALU.add).then_inc(x1_ready, 1)

            def phase3(at):
                h, mlp, o, x1, q = at(0), at(1), at(2), at(3), at(4)
                if is_chunk(h, 2):
                    dve.wait_ge(frstd, 2)
                if h.live and not is_chunk(h, 0):
                    take_h(h)
                if mlp.live:
                    output(o)
                    residual(x1)
                else:
                    residual(x1)
                    output(o)
                if q.live:
                    wait(dve, xqT_ps, q.n - 1)
                    dve.wait_ge(x1_rstd, q.n + 1)
                if x1.live:
                    dve.wait_ge(x1_ready, x1.n + 1)
                    for i in range(G):
                        at_i = x1.buf * G + i
                        last = dve.bn_stats(xstat[:, at_i * 6:at_i * 6 + 6], tile(x1_c, x1, i))
                    last.then_inc(x1_bn, 1)
                if q.live:
                    for i in range(G):
                        m = (q.buf * G + i) * 2
                        last = dve.tensor_scalar(tile(xq_c, q, i), tile(x1_c, q, i), xmv[:, m:m + 1],
                                                 xrstd[:, q.buf * G + i:q.buf * G + i + 1],
                                                 ALU.subtract, ALU.mult, saturate=False)
                    last.then_inc(xq_ready, 1)
                if x1.live:
                    wait(dve, x1_rstd, x1.n - 1)
                    stats_terms(x1, x1_bn, x1_halves)
                if h.live:
                    dve.wait_ge(hi_ready, h.n + 1)
                    dve.tensor_tensor(buf(hTl, h), HT_B[:, :], buf(hTh, h).bitcast(F32),
                                      ALU.subtract).then_inc(lo_ready, 1)
                if x1.live:
                    stats_halves(x1, x1_halves, x1_terms)
                    stats_var(x1, x1_terms, x1_var)

            dve.wait_ge(xb_ready, NC)
            run_steps(dve, NC, 4, phase3)

        @block.tensor
        def _(pe):
            pe.wait_ge(consts, CONSTS)
            pe.wait_ge(wd_in, 16)
            pe.matmul(bank[6][:, 0:D], Wd_raw, centre, start=True, stop=True).then_inc(wd_ps, 1)

            def phase1(at):
                k = at(0)
                if k.live:
                    pe.wait_ge(ctx_sem[k.buf], 16 * (k.pair + 1))
                    wait(pe, vT_sb, k.n - 1)
                    for i in range(G):
                        last = pe.transpose(VT_B[k.buf][:, i * D:(i + 1) * D], tile(ctx_c, k, i), ident[:, :])
                    last.then_inc(vT_ps, 1)
                k = at(1)
                if k.live:
                    if is_chunk(k, 0):
                        pe.wait_ge(wd_sb, 1)
                    pe.wait_ge(vT_sb, k.n + 1)
                    wait(pe, P_sb, k.n - 1)
                    for i in range(G):
                        last = pe.matmul(P_B[k.buf][:, i * D:(i + 1) * D], tile(vT_c, k, i), WdT[:, :],
                                         start=True, stop=True)
                    last.then_inc(P_ps, 1)
                if is_chunk(k, 1):
                    pe.wait_ge(w_in, 16 * 5)
                    for j in range(HB):
                        pe.transpose(bank[3][:, j * D:(j + 1) * D], W1_raw[:, j * D:(j + 1) * D], ident[:, :])
                        last = pe.matmul(bank[4][:, j * D:(j + 1) * D], W2_raw[:, j * D:(j + 1) * D], centre,
                                         start=True, stop=True)
                    last.then_inc(w_ps, 1)

            run_steps(pe, NC, 1, phase1)

            pe.wait_ge(w_sb, 1)
            for j in range(HB):
                last = pe.matmul(bank[5][:, j:j + 1], W1u[:, j * D:(j + 1) * D], b_col[:, :], start=True, stop=True)
            last.then_inc(b1_ps, 1)

            def phase2(at):
                k = at(2)
                if k.live:
                    pe.wait_ge(e_ready, k.n + 1)
                    wait(pe, f_ready, k.n - 1)
                    for i in range(G):
                        o = (i % 2) * EPW
                        last = pe.matmul(EP_B[k.buf][i // 2][:, o:o + D + 1], tile(E_c, k, i),
                                         all_tile(PV, k, i, D + 1, D + 1), start=True, stop=True)
                    last.then_inc(ep_ps, 1)
                k = at(1)
                if k.live:
                    pe.wait_ge(dT_sb, k.n + 1)
                    pe.wait_ge(lT_sb, k.n + 1)
                    wait(pe, e_ready, k.n - 1)
                    for i in range(G):
                        last = pe.matmul(S_B[k.buf][:, i * D:(i + 1) * D], tile(lT_c, k, i), tile(dT_c, k, i),
                                         start=True, stop=True)
                    last.then_inc(s_ps, 1)
                k = at(0)
                if k.live:
                    pe.wait_ge(diff_ready, k.n + 1)
                    wait(pe, dT_sb, k.n)
                    for i in range(G):
                        last = pe.transpose(D_B[:, i * D:(i + 1) * D], tile(diff_c, k, i), ident[:, :])
                    last.then_inc(dT_ps, 1)
                    pe.wait_ge(lr_ready, k.n + 1)
                    wait(pe, lT_sb, k.n)
                    for i in range(G):
                        last = pe.transpose(L_B[:, i * D:(i + 1) * D], ln_tile(1, k, i), ident[:, :])
                    last.then_inc(lT_ps, 1)

            pe.wait_ge(P_sb, NC)
            pe.wait_ge(w_done, 1)
            run_steps(pe, NC, 2, phase2)

            def phase3(at):
                h, m, q = at(0), at(1), at(5)

                def mlp1(j):
                    if m.live:
                        if is_chunk(m, 0) and j == 0:
                            pe.wait_ge(f_ready, NC)
                        if j == 0:
                            pe.wait_ge(hi_ready, m.n + 1)
                            pe.wait_ge(lo_ready, m.n + 1)
                        wait(pe, gelu_ready, HB * m.n + (j - 1))
                        ps = M1_B[j % 2][:, :]
                        w_hi, w_lo = W1h[:, j * P:(j + 1) * P], W1l[:, j * P:(j + 1) * P]
                        pe.matmul(ps, w_hi, buf(hTh, m), start=True, stop=False)
                        pe.matmul(ps, w_hi, buf(hTl, m), start=False, stop=False)
                        pe.matmul(ps, w_lo, buf(hTh, m), start=False, stop=True).then_inc(m1_ps, 1)

                def mlp2(j):
                    if m.live:
                        if j == 0:
                            wait(pe, o_ready, m.n - 1)
                        pe.wait_ge(gelu_ready, HB * m.n + (j + 1))
                        for i in range(G):
                            last = pe.matmul(M2_B[m.buf][:, i * D:(i + 1) * D],
                                             buf(hid_c, m, HB * C)[:, j * C + i * D:j * C + (i + 1) * D],
                                             W2T[:, j * D:(j + 1) * D], start=(j == 0 and i == 0), stop=(j == HB - 1),
                                             skip_group_check=True)
                        if j == HB - 1:
                            last.then_inc(m2_ps, 1)

                mlp1(0)
                mlp1(1)
                if is_chunk(m, 0):
                    pe.wait_ge(wf_q, 1)
                    pe.transpose(bank[7][:, 0:D], wq[1], ident[:, :]).then_inc(wf_ps, 1)
                if q.live:
                    pe.wait_ge(xq_ready, q.n + 1)
                    wait(pe, xqT_sb, q.n)
                if h.live:
                    pe.wait_ge(h_ready, h.n + 1)
                    wait(pe, lo_ready, h.n)
                    wait(pe, hi_ready, h.n)
                    for i in range(G):
                        last = pe.transpose(HT_B[:, i * D:(i + 1) * D], tile(h_c, h, i), ident[:, :])
                    last.then_inc(hT_ps, 1)
                if q.live:
                    for i in range(G):
                        last = pe.matmul(XQ_B[:, i * D:(i + 1) * D], tile(xq_c, q, i), ident8[:, :],
                                         start=True, stop=True)
                    last.then_inc(xqT_ps, 1)
                mlp2(0)
                mlp1(2)
                mlp2(1)
                mlp1(3)
                mlp2(2)
                mlp2(3)
                if q.live:
                    if is_chunk(q, 0):
                        pe.wait_ge(wf_sb, 1)
                    pe.wait_ge(xqT_sb, q.n + 1)
                    wait(pe, r16_ready, q.n)
                    for i in range(G):
                        last = pe.matmul(FF_B[:, i * D:(i + 1) * D], tile(xqT_c, q, i), WfT[:, :],
                                         start=True, stop=True)
                    last.then_inc(ff_ps, 1)

            pe.wait_ge(e_ready, NC)
            run_steps(pe, NC, 5, phase3)


_INS = ['x', 'ctx_1024', 'L0_xattn_W_diff', 'L0_xattn_b_diff', 'L0_xattn_ln_g', 'L0_xattn_ln_b', 'L0_xattn_W1',
        'L0_xattn_b1', 'L0_xattn_W2', 'L0_xattn_b2', 'L0_ffn_weight', 'L0_ffn_bias']


def kernel(**inputs):
    import numpy as _np
    import concourse.bacc as _bacc
    from concourse import mybir as _mybir
    from concourse.bass_utils import run_bass_kernel_spmd as _run

    nc = _bacc.Bacc("TRN2", target_bir_lowering=False, num_devices=1)
    arrays, args = {}, []
    for name in _INS:
        a = _np.ascontiguousarray(inputs[name])
        arrays[f"in_{name}_dram"] = a
        args.append(nc.dram_tensor(f"in_{name}_dram", a.shape, _mybir.dt.from_np(a.dtype), kind="ExternalInput").ap())
    shape = arrays["in_x_dram"].shape
    args.append(nc.dram_tensor("out_0_dram", shape, _mybir.dt.float32, kind="ExternalOutput").ap())
    xattn_ffn_kernel(nc, *args)
    r = _run(nc, [arrays], core_ids=[0])
    return r.results[0]["out_0_dram"]
```
